# Optimizing a Trainium2 kernel written in Bass

```python
import numpy as np
import jax
import jax.numpy as jnp

def _softmax(x, axis=-1):
    return jax.nn.softmax(x, axis=axis)

def _gelu(x):
    return jax.nn.gelu(x, approximate=True)

def _silu(x):
    return jax.nn.silu(x)

def _sigmoid(x):
    return jax.nn.sigmoid(x)

def _layernorm(x, axis=-1, eps=1e-05):
    m = jnp.mean(x, axis=axis, keepdims=True)
    v = jnp.var(x, axis=axis, keepdims=True)
    return (x - m) / jnp.sqrt(v + eps)

def _scatter_add(tgt, idx, src, axis=0):
    return tgt.at[idx].add(src)

def _segment_sum(src, seg, n):
    return jax.ops.segment_sum(src, seg, n)
kernel_name = 'mk_gnn_preln_d2_gnn_r8_d6ea26'

def setup_inputs(seed: int=0):
    np.random.seed(seed)
    _w = jnp.asarray

    def _rec_inputs():
        import jax
        import jax.numpy as jnp
        _gk = jax.random.key(seed)
        x = -0.0001006 + 1 * jax.random.normal(jax.random.fold_in(_gk, 1), (12500, 96), jnp.float32)
        src = jax.random.randint(jax.random.fold_in(_gk, 2), (400000,), 0, 12500, jnp.int32)
        dst = jax.random.randint(jax.random.fold_in(_gk, 3), (400000,), 0, 12500, jnp.int32)
        _o = jnp.argsort(dst, stable=True)
        src = src[_o]
        dst = dst[_o]
        edge_attr_32 = 0.000196303 + 1.00016 * jax.random.normal(jax.random.fold_in(_gk, 11), (400000, 32), jnp.float32)
        edge_weight = jax.random.uniform(jax.random.fold_in(_gk, 13), (400000,), jnp.float32, 0.0, 0.999998)
        return (x, src, dst, edge_attr_32, edge_weight)
    x, src, dst, edge_attr_32, edge_weight = _rec_inputs()

    def _L0_gnn_setup():
        import jax, jax.numpy as jnp
        import numpy as np
        N, E = (6250, 100000)
        ND, ED = (96, 32)

        def _gelu(x):
            return jax.nn.gelu(x, approximate=False)
        key = jax.random.key(seed)
        ks = jax.random.split(key, 16)
        s = lambda fan_in: 1.0 / np.sqrt(fan_in)
        inp = {'x': jax.random.normal(ks[0], (N, ND), jnp.float32), 'edge_index': jax.random.randint(ks[1], (2, E), 0, N, jnp.int32), 'edge_attr': jax.random.normal(ks[2], (E, ED), jnp.float32), 'mW1': jax.random.uniform(ks[3], (ND + ED, ND), jnp.float32, -s(ND + ED), s(ND + ED)), 'mb1': jnp.zeros((ND,), jnp.float32), 'mW2': jax.random.uniform(ks[4], (ND, ND), jnp.float32, -s(ND), s(ND)), 'mb2': jnp.zeros((ND,), jnp.float32), 'gW1': jax.random.uniform(ks[5], (ND + ED, ND), jnp.float32, -s(ND + ED), s(ND + ED)), 'gb1': jnp.zeros((ND,), jnp.float32), 'gW2': jax.random.uniform(ks[6], (ND, 1), jnp.float32, -s(ND), s(ND)), 'gb2': jnp.zeros((1,), jnp.float32), 'uW1': jax.random.uniform(ks[7], (2 * ND, ND), jnp.float32, -s(2 * ND), s(2 * ND)), 'ub1': jnp.zeros((ND,), jnp.float32), 'uW2': jax.random.uniform(ks[8], (ND, ND), jnp.float32, -s(ND), s(ND)), 'ub2': jnp.zeros((ND,), jnp.float32), 'ln_g': jnp.ones((ND,), jnp.float32), 'ln_b': jnp.zeros((ND,), jnp.float32)}
        return inp
    _L0_gnn_all = _L0_gnn_setup()
    _L0_gnn_in = {k: v for k, v in _L0_gnn_all.items() if k in ('mW1', 'mb1', 'mW2', 'mb2', 'gW1', 'gb1', 'gW2', 'gb2', 'uW1', 'ub1', 'uW2', 'ub2', 'ln_g', 'ln_b')}
    del _L0_gnn_all

    def _L1_gnn_setup():
        import jax, jax.numpy as jnp
        import numpy as np
        N = 6250
        E = 100000
        D = 96
        N_LAYER = 2

        def _gcn_conv(x, edge_index, edge_weight, W, b):
            n = x.shape[0]
            h = x @ W
            loop = jnp.arange(n, dtype=edge_index.dtype)
            row = jnp.concatenate([edge_index[0], loop])
            col = jnp.concatenate([edge_index[1], loop])
            w = jnp.concatenate([edge_weight, jnp.ones((n,), h.dtype)])
            deg = jax.ops.segment_sum(w, col, num_segments=n)
            deg_safe = jnp.where(deg > 0, deg, 1.0)
            dinv = jnp.where(deg > 0, jax.lax.rsqrt(deg_safe), 0.0)
            norm = dinv[row] * w * dinv[col]
            msg = norm[:, None] * h[row]
            out = jax.ops.segment_sum(msg, col, num_segments=n)
            return out + b
        key = jax.random.key(seed)
        ks = jax.random.split(key, 12)
        s = 1.0 / np.sqrt(D)
        x = jax.random.normal(ks[0], (N, D), jnp.float32)
        edge_index = jax.random.randint(ks[1], (2, E), 0, N, dtype=jnp.int64)
        edge_weight = jax.random.uniform(ks[2], (E,), jnp.float32)
        return {'x': x, 'edge_index': edge_index, 'edge_weight': edge_weight, 'W0': jax.random.normal(ks[3], (D, D), jnp.float32) * s, 'b0': jnp.zeros((D,), jnp.float32), 'W1': jax.random.normal(ks[4], (D, D), jnp.float32) * s, 'b1': jnp.zeros((D,), jnp.float32), 'Wr0': jax.random.normal(ks[5], (D, D), jnp.float32) * s, 'br0': jax.random.normal(ks[6], (D,), jnp.float32) * 0.01, 'Wr1': jax.random.normal(ks[7], (D, D), jnp.float32) * s, 'br1': jax.random.normal(ks[8], (D,), jnp.float32) * 0.01}
    _L1_gnn_all = _L1_gnn_setup()
    _L1_gnn_in = {k: v for k, v in _L1_gnn_all.items() if k in ('W0', 'b0', 'W1', 'b1', 'Wr0', 'br0', 'Wr1', 'br1')}
    del _L1_gnn_all
    return {'x': x, 'src': src, 'dst': dst, 'edge_attr_32': edge_attr_32, 'edge_weight': edge_weight, 'L0_gnn_mW1': _L0_gnn_in['mW1'], 'L0_gnn_mb1': _L0_gnn_in['mb1'], 'L0_gnn_mW2': _L0_gnn_in['mW2'], 'L0_gnn_mb2': _L0_gnn_in['mb2'], 'L0_gnn_gW1': _L0_gnn_in['gW1'], 'L0_gnn_gb1': _L0_gnn_in['gb1'], 'L0_gnn_gW2': _L0_gnn_in['gW2'], 'L0_gnn_gb2': _L0_gnn_in['gb2'], 'L0_gnn_uW1': _L0_gnn_in['uW1'], 'L0_gnn_ub1': _L0_gnn_in['ub1'], 'L0_gnn_uW2': _L0_gnn_in['uW2'], 'L0_gnn_ub2': _L0_gnn_in['ub2'], 'L0_gnn_ln_g': _L0_gnn_in['ln_g'], 'L0_gnn_ln_b': _L0_gnn_in['ln_b'], 'L1_gnn_W0': _L1_gnn_in['W0'], 'L1_gnn_b0': _L1_gnn_in['b0'], 'L1_gnn_W1': _L1_gnn_in['W1'], 'L1_gnn_b1': _L1_gnn_in['b1'], 'L1_gnn_Wr0': _L1_gnn_in['Wr0'], 'L1_gnn_br0': _L1_gnn_in['br0'], 'L1_gnn_Wr1': _L1_gnn_in['Wr1'], 'L1_gnn_br1': _L1_gnn_in['br1']}

def reference(x, src, dst, edge_attr_32, edge_weight, L0_gnn_mW1, L0_gnn_mb1, L0_gnn_mW2, L0_gnn_mb2, L0_gnn_gW1, L0_gnn_gb1, L0_gnn_gW2, L0_gnn_gb2, L0_gnn_uW1, L0_gnn_ub1, L0_gnn_uW2, L0_gnn_ub2, L0_gnn_ln_g, L0_gnn_ln_b, L1_gnn_W0, L1_gnn_b0, L1_gnn_W1, L1_gnn_b1, L1_gnn_Wr0, L1_gnn_br0, L1_gnn_Wr1, L1_gnn_br1):
    import jax
    import jax.numpy as jnp

    def _L0_gnn_ref(x, edge_index, edge_attr, mW1, mb1, mW2, mb2, gW1, gb1, gW2, gb2, uW1, ub1, uW2, ub2, ln_g, ln_b):
        import jax, jax.numpy as jnp
        import numpy as np
        N, E = (6250, 100000)
        ND, ED = (96, 32)

        def _gelu(x):
            return jax.nn.gelu(x, approximate=False)
        src, dst = (edge_index[0], edge_index[1])
        edge_input = jnp.concatenate([x[src], edge_attr], axis=-1)
        messages = _gelu(edge_input @ mW1 + mb1) @ mW2 + mb2
        gates = jax.nn.sigmoid(_gelu(edge_input @ gW1 + gb1) @ gW2 + gb2)
        aggregated = jax.ops.segment_sum(messages * gates, dst, num_segments=x.shape[0])
        combined = jnp.concatenate([x, aggregated], axis=-1)
        update = _gelu(combined @ uW1 + ub1) @ uW2 + ub2
        h = x + update
        mu = jnp.mean(h, axis=-1, keepdims=True)
        var = jnp.mean(jnp.square(h - mu), axis=-1, keepdims=True)
        return (h - mu) * jax.lax.rsqrt(var + 1e-05) * ln_g + ln_b

    def _L1_gnn_ref(x, edge_index, edge_weight, W0, b0, W1, b1, Wr0, br0, Wr1, br1):
        import jax, jax.numpy as jnp
        import numpy as np
        N = 6250
        E = 100000
        D = 96
        N_LAYER = 2

        def _gcn_conv(x, edge_index, edge_weight, W, b):
            n = x.shape[0]
            h = x @ W
            loop = jnp.arange(n, dtype=edge_index.dtype)
            row = jnp.concatenate([edge_index[0], loop])
            col = jnp.concatenate([edge_index[1], loop])
            w = jnp.concatenate([edge_weight, jnp.ones((n,), h.dtype)])
            deg = jax.ops.segment_sum(w, col, num_segments=n)
            deg_safe = jnp.where(deg > 0, deg, 1.0)
            dinv = jnp.where(deg > 0, jax.lax.rsqrt(deg_safe), 0.0)
            norm = dinv[row] * w * dinv[col]
            msg = norm[:, None] * h[row]
            out = jax.ops.segment_sum(msg, col, num_segments=n)
            return out + b
        layers = ((W0, b0, Wr0, br0), (W1, b1, Wr1, br1))
        for W, b, Wr, br in layers:
            h_in = x
            xc = _gcn_conv(x, edge_index, edge_weight, W, b)
            g = jax.nn.sigmoid(h_in @ Wr + br)
            x = jax.nn.relu((1.0 - g) * h_in + g * xc)
        return x
    edge_index = jnp.stack([src, dst])
    h = jnp.maximum(_layernorm(x, axis=-1), 0.0)
    x = x + _L0_gnn_ref(h, edge_index, edge_attr_32, L0_gnn_mW1, L0_gnn_mb1, L0_gnn_mW2, L0_gnn_mb2, L0_gnn_gW1, L0_gnn_gb1, L0_gnn_gW2, L0_gnn_gb2, L0_gnn_uW1, L0_gnn_ub1, L0_gnn_uW2, L0_gnn_ub2, L0_gnn_ln_g, L0_gnn_ln_b)
    h = jnp.maximum(_layernorm(x, axis=-1), 0.0)
    x = x + _L1_gnn_ref(h, edge_index, edge_weight, L1_gnn_W0, L1_gnn_b0, L1_gnn_W1, L1_gnn_b1, L1_gnn_Wr0, L1_gnn_br0, L1_gnn_Wr1, L1_gnn_br1)
    return x

_drawn_inputs = setup_inputs


def setup_inputs(seed=0):
    import zlib

    import numpy as np

    out = dict(_drawn_inputs(seed))
    spreads = {'L0_gnn_mb1': (0.0, 0.1),
     'L0_gnn_mb2': (0.0, 0.1),
     'L0_gnn_gb1': (0.0, 0.8),
     'L0_gnn_ub1': (0.0, 0.276),
     'L0_gnn_ub2': (0.0, 0.1),
     'L0_gnn_ln_g': (1.0, 0.2),
     'L0_gnn_ln_b': (0.0, 0.1),
     'L1_gnn_b0': (0.0, 0.722),
     'L1_gnn_b1': (0.0, 0.398)}
    factors = {'edge_weight': 30.599,
     'L0_gnn_gW1': 4.739,
     'L0_gnn_gW2': 8.0,
     'L1_gnn_br0': 64.0,
     'L1_gnn_br1': 64.0}
    for name, (base, spread) in spreads.items():
        noise = np.random.default_rng([zlib.crc32(name.encode()), seed]).standard_normal(out[name].shape)
        drawn = base * np.exp(spread * noise) if base else spread * noise
        out[name] = jnp.asarray(drawn.astype(out[name].dtype))
    for name, factor in factors.items():
        out[name] = (out[name] * factor).astype(out[name].dtype)
    return out
```

```python
import contextlib

import concourse.bass as bass
import concourse.mybir as mybir
from concourse.alu_op_type import AluOpType as ALU

F32 = mybir.dt.float32
I32 = mybir.dt.int32
ACT = mybir.ActivationFunctionType
AX = mybir.AxisListType

N = 12500
E = 400000
D = 96
ED = 32
P = 128
EPS = 1e-5

TILES_PER_CHUNK = 7
CHUNK = P * TILES_PER_CHUNK
CHUNKS = -(-N // CHUNK)
NODES = CHUNKS * CHUNK
CF = TILES_PER_CHUNK * D

QUAD = 4
GROUP = 8
QUADS_PER_ITER = 4
GROUPS_PER_ITER = 2
TILES_PER_ITER = QUAD * QUADS_PER_ITER
ITERS = -(-E // (P * TILES_PER_ITER))
QUADS = ITERS * QUADS_PER_ITER
GROUPS = ITERS * GROUPS_PER_ITER
TILES = ITERS * TILES_PER_ITER
EDGES = TILES * P
WINDOW = 64
WINDOW_LOG2 = 6
ACC = NODES + WINDOW
GATE_ROW = D
DEG_ROW = D + 1
ACC_ROWS = D + 2
H2 = 2 * D
GB = GROUPS // 4


class Steps:

    def __init__(self, engine, semaphore, base):
        self.engine, self.semaphore, self.base, self.n = engine, semaphore, base, 0

    def did(self, instruction):
        self.n += 1
        return instruction.then_inc(self.semaphore, 1)

    def wait(self):
        self.engine.wait_ge(self.semaphore, self.base + self.n)


LN_STATS = 6
SRC_STEPS = 7
UPD_SUM, UPD_VAR1 = 2, 8
UPD_X1 = 12
UPD_VAR2 = 18
UPD_H1 = 19
UPD_DEG = 24
UPD_STEPS = 25


def build(nc, io):
    ctx = contextlib.ExitStack()
    with ctx:
        def sb(name, shape, dt=F32):
            return ctx.enter_context(nc.sbuf_tensor(name, shape, dt))

        def ps(name, columns):
            return ctx.enter_context(nc.psum_tensor(name, [P, columns], F32))

        def sem(name):
            return ctx.enter_context(nc.semaphore(name))

        def dram(name, shape):
            return nc.dram_tensor(name, shape, F32).ap()

        src_table = dram("src_table", [CHUNKS, P, TILES_PER_CHUNK * H2])
        conv_table = [dram(f"conv_table{l}", [CHUNKS, P, CF]) for l in range(2)]
        h_src = dram("h_src", [CHUNKS, P, CF])
        x1_keep = dram("x1_keep", [CHUNKS, P, CF])
        h_conv = [dram(f"h_conv{l}", [CHUNKS, P, CF]) for l in range(2)]
        mix_keep = [dram(f"mix_keep{l}", [CHUNKS, P, CF]) for l in range(2)]
        src_rows = src_table.rearrange("c p (k f) -> (c p k) f", f=H2)
        conv_rows = [t.rearrange("c p (k f) -> (c p k) f", f=D) for t in conv_table]

        acc = sb("acc", [P, ACC])
        rel = sb("rel", [P, TILES])
        weight = sb("weight", [P, TILES])
        base_f = sb("base_f", [P, GROUPS])
        base_i = sb("base_i", [1, GROUPS], I32)
        first_base = sb("first_base", [P, GROUPS])
        rounds_i = sb("rounds_i", [1, 1], I32)
        dinv = sb("dinv", [P, CHUNKS * TILES_PER_CHUNK])
        ident = sb("ident", [P, P])
        ones = sb("ones", [P, P])
        w_src = sb("w_src", [D + 1, H2])
        w_attr = sb("w_attr", [ED, H2])
        gate_w2 = sb("gate_w2", [P, D])
        gate_b2 = sb("gate_b2", [P, 1])
        gate_b2_half = sb("gate_b2_half", [P, 1])
        msg_w2_t = sb("msg_w2_t", [D, D + 1])
        upd_top = sb("upd_top", [D, D])
        upd_bottom = sb("upd_bottom", [D, D])
        msg_upd = sb("msg_upd", [D + 1, D])
        upd_b1 = sb("upd_b1", [D, 1])
        upd_w2 = sb("upd_w2", [D + 1, D])
        ln_g = sb("ln_g", [P, D])
        ln_b = sb("ln_b", [P, D])
        conv_w = [sb(f"conv_w{l}", [D + 1, H2]) for l in range(2)]
        conv_b = [sb(f"conv_b{l}", [P, D]) for l in range(2)]
        act_warm = sb("act_warm", [P, 1])

        x_c = sb("x_c", [P, CF])
        h_c = sb("h_c", [P, CF])
        t_c = sb("t_c", [P, CF])
        q_c = sb("q_c", [P, CF])
        m_c = sb("m_c", [P, CF])
        s_c = sb("s_c", [P, TILES_PER_CHUNK * H2])
        h_t = sb("h_t", [D + 1, CHUNK])
        u_t = sb("u_t", [D + 1, CHUNK])
        acc_t = sb("acc_t", [ACC_ROWS, CHUNK])
        st = sb("st", [P, 8, TILES_PER_CHUNK])
        rstd = sb("rstd", [P, TILES_PER_CHUNK])
        neg_half = sb("neg_half", [P, TILES_PER_CHUNK])
        src_ids = [sb(f"src_ids{b}", [P, GROUP], I32) for b in range(GROUPS_PER_ITER)]
        attr = [sb(f"attr{b}", [ED, GROUP * P]) for b in range(GROUPS_PER_ITER)]
        hid = [sb(f"hid{s}", [P, QUAD, H2]) for s in range(QUADS_PER_ITER)]
        prod = sb("prod", [P, QUAD, D])
        logit = [sb(f"logit{b}", [P, QUAD]) for b in range(2)]
        gate_t = [sb(f"gate_t{b}", [P, QUAD]) for b in range(2)]
        msg = [sb(f"msg{b}", [P, QUAD, ACC_ROWS]) for b in range(2)]
        hot = [sb(f"hot{b}", [P, QUAD, WINDOW]) for b in range(2)]
        conv_g = [sb(f"conv_g{b}", [P, GROUP, D]) for b in range(2)]
        conv_s = [sb(f"conv_s{b}", [P, GROUP, WINDOW]) for b in range(2)]
        dst_i = sb("dst_i", [P, TILES], I32)
        iota_i = sb("iota_i", [P, WINDOW], I32)
        lim = sb("lim", [P, 2, GROUPS])
        lim_g = sb("lim_g", [GB, 8, 4])
        diag = sb("diag", [GB, 4, GB])
        span = sb("span", [GB, 2])
        top = sb("top", [1, 2])
        top_i = sb("top_i", [1, 2], I32)

        pa = ps("pa", 1024)
        pb = ps("pb", 1024)
        sg = [ps("sg0", 512), ps("sg1", 512)]
        px = ps("px", 512)
        const = ps("const", 512)
        iota = const[:, 0:WINDOW]
        gate_w2_ps = const[:, WINDOW:WINDOW + D]
        attr_ps = [pa, pb]

        s_weights = sem("weights_in")
        s_edges = sem("edges_in")
        s_pool_const = sem("pool_const")
        s_setup = sem("setup_steps")
        s_setup_pe = sem("setup_pe")
        s_ready = sem("setup_ready")
        s_bias = sem("bias_ready")
        s_x_in = sem("x_in")
        s_src = sem("src_steps")
        s_src_pow = sem("src_pow")
        s_src_t = sem("src_transposed")
        s_src_ht = sem("src_ht")
        s_src_mm = sem("src_product")
        s_src_ev = sem("src_copied")
        s_h_out = sem("h_out")
        s_table_out = sem("table_out")
        s_ids = [sem(f"ids_in{b}") for b in range(GROUPS_PER_ITER)]
        s_attr = [sem(f"attr_in{b}") for b in range(GROUPS_PER_ITER)]
        s_gath = [sem(f"gathered{s}") for s in range(QUADS_PER_ITER)]
        s_attr_mm = sem("attr_product")
        s_added = sem("added")
        s_gelu = sem("gelu_done")
        s_prod = sem("gate_products")
        s_dotted = sem("gate_logits")
        s_tanh = sem("tanh_done")
        s_gcol = sem("gate_columns")
        s_gated = sem("gated")
        s_seg = sem("segment_sums")
        s_acc = sem("accumulated")
        s_shift = sem("windows_moved")
        s_back = [sem(f"rel_back{p}") for p in range(3)]
        s_window = sem("windows_back")
        s_passed = sem("passed")
        s_acc0 = [sem(f"acc_zeroed{p}") for p in range(3)]
        s_up_in = sem("upd_in")
        s_up_x = sem("upd_x_in")
        s_up_t = sem("upd_transposed")
        s_up_ht = sem("upd_ht")
        s_up_acc = sem("upd_acc_copied")
        s_up_u = sem("upd_hidden")
        s_up_g = sem("upd_gelu")
        s_up_mm = sem("upd_product")
        s_up = sem("upd_steps")
        s_up_pow = sem("upd_pow")
        s_x1_out = sem("x1_out")
        s_h1_out = sem("h1_out")
        pr = [{k: sem(f"proj{l}_{k}") for k in
               ("h_in", "t", "ht", "mm", "scaled", "tanh", "mixed", "table_out", "mix_out")} for l in range(2)]
        cv = [{k: sem(f"conv{l}_{k}") for k in
               ("ids0", "ids1", "gath0", "gath1", "hot", "weighted", "seg", "acc", "shift")} for l in range(2)]
        cb = [{k: sem(f"comb{l}_{k}") for k in
               ("h_in", "m_in", "q_in", "x_in", "acc_t", "t", "steps", "out")} for l in range(2)]

        block = ctx.enter_context(nc.Block())

        def tiles(ap, f=D):
            return ap.rearrange("p (k f) -> p k f", f=f)

        def per_node(ap):
            return ap.unsqueeze(2).to_broadcast([P, TILES_PER_CHUNK, D])

        def per_feature(ap, k=TILES_PER_CHUNK):
            return ap.unsqueeze(1).to_broadcast([P, k, D])

        def chunk(t, c):
            return t[bass.ds(c, 1), :, :].rearrange("o p f -> (o p) f")

        def acc_chunk(c, rows):
            return acc[0:rows, bass.ds(c * CHUNK, CHUNK)].rearrange("r (p k) -> r k p", k=TILES_PER_CHUNK)

        def tile_cols(t, k, rows):
            return t[0:rows, k * P:(k + 1) * P]

        def table_slot(k):
            if k < 4:
                return pb[:, 512 * (k // 2) + H2 * (k % 2):512 * (k // 2) + H2 * (k % 2 + 1)]
            return sg[(k - 4) // 2][:, H2 * (k % 2):H2 * (k % 2 + 1)]

        TABLE_SLOTS = [(pb[:, 0:2 * H2], 0, 2), (pb[:, 512:512 + 2 * H2], 2, 2),
                       (sg[0][:, 0:2 * H2], 4, 2), (sg[1][:, 0:H2], 6, 1)]
        NODE_SLOTS = [(sg[0], 0, 4), (sg[1], 4, 3)]

        def node_slot(k):
            bank = sg[0] if k < 4 else sg[1]
            return bank[:, D * (k % 4):D * (k % 4 + 1)]

        def over_chunks(eng, body):
            body(0, True)
            with eng.Fori(1, CHUNKS) as c:
                body(c, False)

        def wait_apart(eng, semaphore, value):
            eng.wait_ge(semaphore, value)
            if not isinstance(value, int):
                eng.sem_inc(s_passed, 1)

        def load_rounds(eng):
            return eng.value_load(rounds_i[0:1, 0:1], min_val=1, max_val=N // WINDOW + 1)

        def edge_pass(eng, rounds, iteration, round_end):
            with eng.Fori(0, rounds) as r:
                n0 = eng.snap(r * ITERS)
                iteration(0, n0, True, False)
                with eng.Fori(1, ITERS - 1) as it:
                    iteration(it, n0 + it, False, False)
                iteration(ITERS - 1, n0 + (ITERS - 1), False, True)
                round_end(r)

        def transposes(src):
            for k in range(TILES_PER_CHUNK):
                last = nc.tensor.transpose(pa[0:D, 512 * (k // 4) + P * (k % 4):512 * (k // 4) + P * (k % 4 + 1)],
                                           src[:, k * D:(k + 1) * D], ident[:, :])
            return last

        def table_products(w):
            for k in range(TILES_PER_CHUNK):
                last = nc.tensor.matmul(table_slot(k), tile_cols(h_t, k, D + 1), w[:, :], start=True, stop=True)
            return last

        @block.sync
        def _(sp):
            for name, t in (("w_src", w_src), ("w_attr", w_attr), ("msg_w2_t", msg_w2_t), ("upd_top", upd_top),
                            ("upd_bottom", upd_bottom), ("upd_b1", upd_b1), ("upd_w2", upd_w2),
                            ("conv_w0", conv_w[0]), ("conv_w1", conv_w[1])):
                sp.dma_start(t[:, :], io[name]).then_inc(s_weights, 16)
            for name, t in (("gate_w2", gate_w2), ("gate_b2", gate_b2), ("ln_g", ln_g), ("ln_b", ln_b),
                            ("conv_b0", conv_b[0]), ("conv_b1", conv_b[1])):
                sp.dma_start(t[:, :], io[name].partition_broadcast(P)).then_inc(s_weights, 16)
            sp.dma_start(dst_i[:, :], io["dst"]).then_inc(s_edges, 16)
            sp.dma_start(weight[:, :], io["weight"]).then_inc(s_edges, 16)

            sp.dma_start(x_c[:, :], chunk(io["x"], 0)).then_inc(s_x_in, 16)

            def source(c, first, last=False):
                sp.wait_ge(s_src, c * SRC_STEPS + SRC_STEPS)
                sp.dma_start(chunk(h_src, c), h_c[:, :]).then_inc(s_h_out, 16)
                if not last:
                    sp.dma_start(x_c[:, :], chunk(io["x"], c + 1)).then_inc(s_x_in, 16)
                sp.wait_ge(s_src_ev, 4 * c + 4)
                sp.dma_start(chunk(src_table, c), s_c[:, :]).then_inc(s_table_out, 16)

            source(0, True)
            with sp.Fori(1, CHUNKS - 1) as c:
                source(c, False)
            source(CHUNKS - 1, False, True)

            sp.wait_ge(s_ready, 1)
            rounds = load_rounds(sp)

            def edges(it, n, first, last):
                for b in range(GROUPS_PER_ITER):
                    if not first:
                        sp.wait_ge(s_gath[2 * b], QUAD * 16 * n)
                        sp.wait_ge(s_gath[2 * b + 1], QUAD * 16 * n)
                    sp.dma_start(src_ids[b][:, :], chunk(io["src"], it * 2 + b)).then_inc(s_ids[b], 16)
                    if not first:
                        sp.wait_ge(s_attr_mm, QUADS_PER_ITER * (n - 1) + 2 * b + 2)
                    sp.dma_start(attr[b][:, :], chunk(io["attr"], it * 2 + b)).then_inc(s_attr[b], 16)

            edge_pass(sp, rounds, edges, lambda r: wait_apart(sp, s_acc, r * GROUPS + GROUPS))

            sp.wait_ge(s_h_out, 16 * CHUNKS)

            def update(c, first):
                if not first:
                    wait_apart(sp, s_up, UPD_STEPS * c)
                    sp.wait_ge(s_h1_out, 16 * c)
                    sp.wait_ge(s_x1_out, 16 * c)
                    sp.wait_ge(s_up_t, c)
                sp.dma_start(h_c[:, :], chunk(h_src, c)).then_inc(s_up_in, 16)
                sp.dma_start(x_c[:, :], chunk(io["x"], c)).then_inc(s_up_x, 16)
                sp.wait_ge(s_up, UPD_STEPS * c + UPD_X1)
                sp.dma_start(chunk(x1_keep, c), x_c[:, :]).then_inc(s_x1_out, 16)
                sp.wait_ge(s_up, UPD_STEPS * c + UPD_H1)
                sp.dma_start(chunk(h_conv[0], c), q_c[:, :]).then_inc(s_h1_out, 16)

            over_chunks(sp, update)
            sp.wait_ge(s_h1_out, 16 * CHUNKS)
            sp.wait_ge(s_x1_out, 16 * CHUNKS)
            sp.wait_ge(s_up, UPD_STEPS * CHUNKS)

            for l in range(2):
                def project(c, first, s=pr[l], l=l):
                    if not first:
                        sp.wait_ge(s["t"], c)
                    sp.dma_start(h_c[:, :], chunk(h_conv[l], c)).then_inc(s["h_in"], 16)
                    sp.wait_ge(s["scaled"], 4 * c + 4)
                    sp.dma_start(chunk(conv_table[l], c), q_c[:, :]).then_inc(s["table_out"], 16)
                    sp.wait_ge(s["mixed"], c + 1)
                    sp.dma_start(chunk(mix_keep[l], c), m_c[:, :]).then_inc(s["mix_out"], 16)

                over_chunks(sp, project)

                def conv_edges(it, n, first, last, s=cv[l]):
                    for b in range(GROUPS_PER_ITER):
                        if not first:
                            sp.wait_ge(s[f"gath{b}"], GROUP * 16 * n)
                        sp.dma_start(src_ids[b][:, :], chunk(io["src"], it * 2 + b)).then_inc(s[f"ids{b}"], 16)

                edge_pass(sp, rounds, conv_edges, lambda r, s=cv[l]: wait_apart(sp, s["acc"], r * GROUPS + GROUPS))

                sp.wait_ge(pr[l]["table_out"], 16 * CHUNKS)
                sp.wait_ge(pr[l]["mix_out"], 16 * CHUNKS)

                def combine(c, first, s=cb[l], l=l):
                    steps = COMBINE_STEPS[l]
                    if not first:
                        wait_apart(sp, s["steps"], steps * c)
                        sp.wait_ge(s["out"], 16 * c)
                    sp.dma_start(q_c[:, :], chunk(conv_table[l], c)).then_inc(s["q_in"], 16)
                    sp.dma_start(h_c[:, :], chunk(h_conv[l], c)).then_inc(s["h_in"], 16)
                    sp.dma_start(m_c[:, :], chunk(mix_keep[l], c)).then_inc(s["m_in"], 16)
                    if l == 1:
                        sp.dma_start(x_c[:, :], chunk(x1_keep, c)).then_inc(s["x_in"], 16)
                    sp.wait_ge(s["steps"], steps * c + steps)
                    sp.dma_start(chunk(h_conv[1] if l == 0 else io["out"], c), t_c[:, :]).then_inc(s["out"], 16)

                over_chunks(sp, combine)
                sp.wait_ge(cb[l]["out"], 16 * CHUNKS)

        @block.gpsimd
        def _(pool):
            do = Steps(pool, s_pool_const, 0)
            for fill in (lambda: pool.memset(ident[:, :], 0.0),
                         lambda: pool.affine_select(out=ident[:, :], in_=ident[:, :], compare_op=ALU.not_equal,
                                                    fill=1.0, base=0, pattern=[[-1, P]], channel_multiplier=1),
                         lambda: pool.memset(ones[:, :], 1.0),
                         lambda: pool.iota(iota_i[:, :], pattern=[[1, WINDOW]], base=0, channel_multiplier=0),
                         lambda: pool.memset(h_t[D:D + 1, :], 1.0),
                         lambda: pool.memset(u_t[D:D + 1, :], 1.0),
                         lambda: pool.memset(neg_half[:, :], -0.5)):
                do.did(fill())
                do.wait()
            pool.memset(acc[:, :], 0.0).then_inc(s_acc0[0], 1)
            pool.wait_ge(s_acc0[0], 1)

            def inverse_root(src, out):
                return pool.tensor_tensor(out, src, neg_half[:, :], ALU.pow)

            def source(c, first):
                pool.wait_ge(s_src, c * SRC_STEPS + LN_STATS)
                inverse_root(st[:, 3, :], rstd[:, :]).then_inc(s_src_pow, 1)

            over_chunks(pool, source)

            pool.wait_ge(s_ready, 1)
            rounds = load_rounds(pool)
            pool.wait_ge(s_table_out, 16 * CHUNKS)

            def gather(it, n, first, last):
                for s in range(QUADS_PER_ITER):
                    if s % 2 == 0:
                        wait_apart(pool, s_ids[s // 2], 16 * n + 16)
                    if not first:
                        wait_apart(pool, s_gated, QUADS_PER_ITER * (n - 1) + s + 1)
                    for t in range(QUAD):
                        j = QUAD * (s % 2) + t
                        pool.indirect_dma_start(
                            out=hid[s][:, t, :], out_offset=None, in_=src_rows,
                            in_offset=bass.IndirectOffsetOnAxis(ap=src_ids[s // 2][:, j:j + 1], axis=0),
                        ).then_inc(s_gath[s], 16)

            edge_pass(pool, rounds, gather, lambda r: wait_apart(pool, s_acc, r * GROUPS + GROUPS))

            def update(c, first):
                pool.wait_ge(s_up, UPD_STEPS * c + UPD_VAR1)
                inverse_root(st[:, 3, :], rstd[:, :]).then_inc(s_up_pow, 1)
                pool.wait_ge(s_up, UPD_STEPS * c + UPD_VAR2)
                inverse_root(st[:, 3, :], rstd[:, :]).then_inc(s_up_pow, 1)
                pool.wait_ge(s_up, UPD_STEPS * c + UPD_DEG)
                inverse_root(st[:, 6, :], rstd[:, :]).then_inc(s_up_pow, 1)

            over_chunks(pool, update)

            for l in range(2):
                if l == 0:
                    pool.wait_ge(s_up_acc, CHUNKS)
                else:
                    pool.wait_ge(cb[0]["acc_t"], CHUNKS)
                pool.memset(acc[0:D, :], 0.0).then_inc(s_acc0[l + 1], 1)
                pool.wait_ge(pr[l]["table_out"], 16 * CHUNKS)

                def conv_gather(it, n, first, last, s=cv[l], l=l):
                    for b in range(GROUPS_PER_ITER):
                        wait_apart(pool, s[f"ids{b}"], 16 * n + 16)
                        if not first:
                            wait_apart(pool, s["seg"], GROUPS_PER_ITER * (n - 1) + b + 1)
                        for t in range(GROUP):
                            pool.indirect_dma_start(
                                out=conv_g[b][:, t, :], out_offset=None, in_=conv_rows[l],
                                in_offset=bass.IndirectOffsetOnAxis(ap=src_ids[b][:, t:t + 1], axis=0),
                            ).then_inc(s[f"gath{b}"], 16)

                edge_pass(pool, rounds, conv_gather,
                          lambda r, s=cv[l]: wait_apart(pool, s["acc"], r * GROUPS + GROUPS))

        @block.tensor
        def _(pe):
            pe.wait_ge(s_pool_const, 7)
            pe.wait_ge(s_weights, 16 * 15)
            nc.tensor.matmul(px[0:D + 1, 400:400 + D], msg_w2_t[:, :], upd_bottom[:, :],
                             start=True, stop=True).then_inc(s_setup_pe, 1)
            pe.wait_ge(s_setup, 4)
            for m, bank in ((0, pa), (1, pb)):
                for q in range(4):
                    last = nc.tensor.transpose(bank[0:GB, P * q:P * (q + 1)],
                                               lim[:, m, GB * q:GB * (q + 1)], ident[:, :])
            last.then_inc(s_setup_pe, 1)
            pe.wait_ge(s_setup, 12)
            nc.tensor.matmul(sg[0][0:1, 0:GB], span[:, 0:1], ident[0:GB, 0:GB], start=True, stop=True)
            for q in range(4):
                last = nc.tensor.matmul(sg[1][:, GB * q:GB * (q + 1)], ones[0:GB, :], diag[:, q, :],
                                        start=True, stop=True)
            last.then_inc(s_setup_pe, 1)

            pe.wait_ge(s_ready, 1)

            def source(c, first):
                pe.wait_ge(s_src, c * SRC_STEPS + SRC_STEPS)
                if not first:
                    pe.wait_ge(s_src_ht, 2 * c)
                transposes(h_c).then_inc(s_src_t, 1)
                pe.wait_ge(s_src_ht, 2 * c + 2)
                if not first:
                    pe.wait_ge(s_src_ev, 4 * c)
                table_products(w_src).then_inc(s_src_mm, 1)

            over_chunks(pe, source)

            rounds = load_rounds(pe)
            pe.wait_ge(s_src_ev, 4 * CHUNKS)

            def attr_product(n, s, free):
                if s % 2 == 0:
                    pe.wait_ge(s_attr[s // 2], 16 * n + 16)
                if free:
                    pe.wait_ge(s_added, QUADS_PER_ITER * n + s - 1)
                for t in range(QUAD):
                    col = P * (QUAD * (s % 2) + t)
                    last = nc.tensor.matmul(
                        attr_ps[s % 2][:, 512 * (t // 2) + H2 * (t % 2):512 * (t // 2) + H2 * (t % 2 + 1)],
                        attr[s // 2][:, col:col + P], w_attr[:, :], start=True, stop=True)
                last.then_inc(s_attr_mm, 1)

            def edges(it, n, first, last):
                if first:
                    for s in range(3):
                        attr_product(n, s, s == 2)
                for s in range(QUADS_PER_ITER):
                    if s + 3 < QUADS_PER_ITER:
                        attr_product(n, s + 3, True)
                    elif not last:
                        attr_product(n + 1, s + 3 - QUADS_PER_ITER, True)
                    pe.wait_ge(s_gated, QUADS_PER_ITER * n + s + 1)
                    if s % 2 == 0 and not first:
                        pe.wait_ge(s_acc, GROUPS_PER_ITER * (n - 1) + s // 2 + 1)
                    for t in range(QUAD):
                        op = nc.tensor.matmul(sg[s // 2][0:ACC_ROWS, 0:WINDOW], msg[s % 2][:, t, :],
                                              hot[s % 2][:, t, :], start=(s % 2 == 0 and t == 0),
                                              stop=(s % 2 == 1 and t == QUAD - 1))
                    op.then_inc(s_seg, 1)

            edge_pass(pe, rounds, edges, lambda r: pe.wait_ge(s_acc, r * GROUPS + GROUPS))

            def update(c, first):
                pe.wait_ge(s_up_in, 16 * c + 16)
                if not first:
                    pe.wait_ge(s_up_ht, 2 * c)
                transposes(h_c).then_inc(s_up_t, 1)
                pe.wait_ge(s_up_ht, 2 * c + 2)
                pe.wait_ge(s_up_acc, c + 1)
                if not first:
                    pe.wait_ge(s_up_g, 2 * c)
                for k0, k1 in ((0, 4), (4, 7)):
                    out = pb[0:D, 128 * k0:128 * k1]
                    nc.tensor.matmul(out, upd_top[:, :], h_t[0:D, P * k0:P * k1], start=True, stop=False)
                    last = nc.tensor.matmul(out, msg_upd[:, :], acc_t[0:D + 1, P * k0:P * k1], start=False, stop=True)
                last.then_inc(s_up_u, 1)
                pe.wait_ge(s_up_g, 2 * c + 2)
                if not first:
                    pe.wait_ge(s_up, UPD_STEPS * (c - 1) + UPD_DEG)
                for k in range(TILES_PER_CHUNK):
                    nc.tensor.matmul(node_slot(k), tile_cols(u_t, k, D + 1), upd_w2[:, :], start=True, stop=True)
                for k in range(TILES_PER_CHUNK):
                    last = nc.tensor.matmul(px[:, k:k + 1], tile_cols(acc_t, k, ACC_ROWS),
                                            ident[0:ACC_ROWS, DEG_ROW:DEG_ROW + 1], start=True, stop=True)
                last.then_inc(s_up_mm, 1)

            over_chunks(pe, update)
            pe.wait_ge(s_up, UPD_STEPS * CHUNKS)

            for l in range(2):
                def project(c, first, s=pr[l], l=l):
                    pe.wait_ge(s["h_in"], 16 * c + 16)
                    if not first:
                        pe.wait_ge(s["ht"], 2 * c)
                    transposes(h_c).then_inc(s["t"], 1)
                    pe.wait_ge(s["ht"], 2 * c + 2)
                    if not first:
                        pe.wait_ge(s["scaled"], 4 * c)
                        pe.wait_ge(s["tanh"], 4 * c)
                    table_products(conv_w[l]).then_inc(s["mm"], 1)

                over_chunks(pe, project)
                pe.wait_ge(pr[l]["scaled"], 4 * CHUNKS)
                pe.wait_ge(pr[l]["tanh"], 4 * CHUNKS)

                def conv_edges(it, n, first, last, s=cv[l]):
                    for b in range(GROUPS_PER_ITER):
                        pe.wait_ge(s[f"gath{b}"], GROUP * 16 * n + GROUP * 16)
                        pe.wait_ge(s["weighted"], GROUPS_PER_ITER * n + b + 1)
                        if not first:
                            pe.wait_ge(s["acc"], GROUPS_PER_ITER * (n - 1) + b + 1)
                        for t in range(GROUP):
                            op = nc.tensor.matmul(sg[b][0:D, 0:WINDOW], conv_g[b][:, t, :], conv_s[b][:, t, :],
                                                  start=(t == 0), stop=(t == GROUP - 1))
                        op.then_inc(s["seg"], 1)

                edge_pass(pe, rounds, conv_edges, lambda r, s=cv[l]: pe.wait_ge(s["acc"], r * GROUPS + GROUPS))

                def combine(c, first, s=cb[l], l=l):
                    pe.wait_ge(s["acc_t"], c + 1)
                    if not first:
                        pe.wait_ge(s["steps"], COMBINE_STEPS[l] * (c - 1) + 2)
                    for k in range(TILES_PER_CHUNK):
                        last = nc.tensor.transpose(node_slot(k), tile_cols(acc_t, k, D), ident[0:D, 0:D])
                    last.then_inc(s["t"], 1)

                over_chunks(pe, combine)
                pe.wait_ge(cb[l]["steps"], COMBINE_STEPS[l] * CHUNKS)

        @block.scalar
        def _(act):
            act.wait_ge(s_pool_const, 7)
            nc.scalar.activation(act_warm[:, :], ones[:, 0:1], ACT.Gelu).then_inc(s_bias, 1)
            act.wait_ge(s_weights, 16 * 15)
            nc.scalar.activation(gate_b2_half[:, :], gate_b2[:, :], ACT.Copy, scale=0.5).then_inc(s_bias, 1)
            act.wait_ge(s_setup_pe, 1)
            nc.scalar.activation(msg_upd[:, :], px[0:D + 1, 400:400 + D], ACT.Copy).then_inc(s_bias, 1)
            act.wait_ge(s_bias, 3)

            def copy_transposed(semaphore):
                nc.scalar.activation(h_t[0:D, 0:512], pa[0:D, 0:512], ACT.Copy).then_inc(semaphore, 1)
                nc.scalar.activation(h_t[0:D, 512:CHUNK], pa[0:D, 512:CHUNK], ACT.Copy).then_inc(semaphore, 1)

            def source(c, first):
                act.wait_ge(s_src_t, c + 1)
                if not first:
                    act.wait_ge(s_src_mm, c)
                copy_transposed(s_src_ht)
                act.wait_ge(s_src_mm, c + 1)
                if not first:
                    act.wait_ge(s_table_out, 16 * c)
                for bank, k, m in TABLE_SLOTS:
                    nc.scalar.activation(s_c[:, H2 * k:H2 * (k + m)], bank, ACT.Copy).then_inc(s_src_ev, 1)

            over_chunks(act, source)

            act.wait_ge(s_ready, 1)
            rounds = load_rounds(act)

            def gelu(n, s):
                act.wait_ge(s_added, QUADS_PER_ITER * n + s + 1)
                flat = hid[s][:, :, :].rearrange("p t f -> p (t f)")
                nc.scalar.activation(flat, flat, ACT.Gelu).then_inc(s_gelu, 1)

            def tanh(n, s, free):
                act.wait_ge(s_dotted, QUADS_PER_ITER * n + s + 1)
                if free:
                    act.wait_ge(s_gated, QUADS_PER_ITER * n + s - 1)
                nc.scalar.activation(gate_t[s % 2][:, :], logit[s % 2][:, :], ACT.Tanh,
                                     bias=gate_b2_half[:, 0:1], scale=0.5).then_inc(s_tanh, 1)

            def edges(it, n, first, last):
                if first:
                    gelu(n, 0)
                    gelu(n, 1)
                    tanh(n, 0, False)
                for s in range(QUADS_PER_ITER):
                    if s + 2 < QUADS_PER_ITER:
                        gelu(n, s + 2)
                    elif not last:
                        gelu(n + 1, s + 2 - QUADS_PER_ITER)
                    if s + 1 < QUADS_PER_ITER:
                        tanh(n, s + 1, not (first and s == 0))
                    elif not last:
                        tanh(n + 1, 0, True)

            edge_pass(act, rounds, edges, lambda r: act.wait_ge(s_acc, r * GROUPS + GROUPS))

            def update(c, first):
                if not first:
                    act.wait_ge(s_up_mm, c)
                nc.scalar.activation(acc_t[:, :].rearrange("r (k p) -> r k p", p=P), acc_chunk(c, ACC_ROWS),
                                     ACT.Copy).then_inc(s_up_acc, 1)
                act.wait_ge(s_up_t, c + 1)
                copy_transposed(s_up_ht)
                act.wait_ge(s_up_u, c + 1)
                for a, b in ((0, 512), (512, CHUNK)):
                    nc.scalar.activation(u_t[0:D, a:b], pb[0:D, a:b], ACT.Gelu, bias=upd_b1[:, 0:1]).then_inc(s_up_g, 1)

            over_chunks(act, update)
            act.wait_ge(s_up_mm, CHUNKS)

            for l in range(2):
                def project(c, first, s=pr[l]):
                    act.wait_ge(s["t"], c + 1)
                    if not first:
                        act.wait_ge(s["mm"], c)
                    copy_transposed(s["ht"])
                    act.wait_ge(s["mm"], c + 1)
                    if not first:
                        act.wait_ge(s["mix_out"], 16 * c)
                    for bank, k, m in TABLE_SLOTS:
                        nc.scalar.activation(tiles(m_c[:, D * k:D * (k + m)]), tiles(bank, H2)[:, :, D:H2],
                                             ACT.Tanh, scale=0.5).then_inc(s["tanh"], 1)
                    act.wait_ge(s["tanh"], 4 * c + 4)
                    nc.scalar.activation(m_c[:, :], m_c[:, :], ACT.Copy, scale=0.5, bias=0.5).then_inc(s["mixed"], 1)

                over_chunks(act, project)

                act.wait_ge(s_acc0[l + 1], 1)
                with act.Fori(0, rounds) as r:
                    act.wait_ge(cv[l]["acc"], r * GROUPS + GROUPS)

                def combine(c, first, s=cb[l]):
                    if not first:
                        act.wait_ge(s["t"], c)
                    nc.scalar.activation(acc_t[0:D, :].rearrange("r (k p) -> r k p", p=P), acc_chunk(c, D),
                                         ACT.Copy).then_inc(s["acc_t"], 1)

                over_chunks(act, combine)
                act.wait_ge(cb[l]["t"], CHUNKS)

        @block.vector
        def _(dve):
            v = nc.vector

            def layer_norm_stats(do, src, centred, squares):
                do.did(v.tensor_reduce(st[:, 0, :], tiles(src), AX.X, ALU.add))
                do.wait()
                do.did(v.tensor_scalar(st[:, 1, :], st[:, 0, :], -1.0 / D, None, ALU.mult))
                do.wait()
                do.did(v.tensor_tensor(tiles(centred), tiles(src), per_node(st[:, 1, :]), ALU.add))
                do.wait()
                do.did(v.tensor_tensor(squares, centred, centred, ALU.mult))
                do.wait()
                do.did(v.tensor_reduce(st[:, 2, :], tiles(squares), AX.X, ALU.add))
                do.wait()
                do.did(v.tensor_scalar(st[:, 3, :], st[:, 2, :], 1.0 / D, EPS, ALU.mult, ALU.add))

            do = Steps(dve, s_setup, 0)
            dve.wait_ge(s_edges, 32)
            do.did(v.tensor_copy(rel[:, :], dst_i[:, :]))
            do.wait()
            by_group = rel[:, :].rearrange("p (g t) -> p g t", t=GROUP)
            do.did(v.tensor_reduce(lim[:, 0, :], by_group, AX.X, ALU.min))
            masked = dst_i[:, :].bitcast(F32)
            do.did(v.scalar_tensor_tensor(out=masked, in0=rel[:, :], scalar=float(N), in1=rel[:, :],
                                          op0=ALU.is_lt, op1=ALU.mult))
            do.wait()
            do.did(v.tensor_reduce(lim[:, 1, :], masked.rearrange("p (g t) -> p g t", t=GROUP), AX.X, ALU.max))
            dve.wait_ge(s_setup_pe, 2)
            do.did(v.tensor_reduce(lim_g[:, 0, :], pa[0:GB, 0:512].rearrange("g (q p) -> g q p", p=P), AX.X, ALU.min))
            do.did(v.tensor_reduce(lim_g[:, 1, :], pb[0:GB, 0:512].rearrange("g (q p) -> g q p", p=P), AX.X, ALU.max))
            do.wait()
            do.did(v.tensor_tensor(lim_g[:, 2, :], lim_g[:, 1, :], lim_g[:, 0, :], ALU.subtract))
            do.wait()
            do.did(v.tensor_reduce(span[:, 0:1], lim_g[:, 2, :], AX.X, ALU.max))
            dve.wait_ge(s_pool_const, 7)
            for q in range(4):
                do.did(v.tensor_scalar(diag[:, q, :], ident[0:GB, 0:GB], lim_g[:, 0, q:q + 1], None, ALU.mult))
            dve.wait_ge(s_setup_pe, 3)
            do.did(v.tensor_reduce(top[:, 0:1], sg[0][0:1, 0:GB], AX.X, ALU.max))
            do.did(v.tensor_copy(base_f[:, :], sg[1][:, 0:GROUPS]))
            do.wait()
            do.did(v.tensor_scalar(top[:, 1:2], top[:, 0:1], 0.0, None, ALU.max))
            do.did(v.tensor_copy(base_i[:, :], base_f[0:1, :]))
            do.did(v.tensor_copy(first_base[:, :], base_f[:, :]))
            do.did(v.tensor_tensor(by_group, by_group,
                                   base_f[:, :].unsqueeze(2).to_broadcast([P, GROUPS, GROUP]), ALU.subtract))
            do.wait()
            do.did(v.tensor_copy(top_i[:, 0:1], top[:, 1:2]))
            do.wait()
            do.did(v.tensor_scalar(top_i[:, 1:2], top_i[:, 0:1], WINDOW_LOG2, None, ALU.arith_shift_right))
            do.wait()
            do.did(v.tensor_scalar(rounds_i[:, :], top_i[:, 1:2], 1, None, ALU.add))
            do.did(v.tensor_copy(iota, iota_i[:, :]))
            dve.wait_ge(s_weights, 16 * 15)
            do.wait()
            v.tensor_copy(gate_w2_ps, gate_w2[:, :]).then_inc(s_ready, 1)

            def source(c, first):
                do = Steps(dve, s_src, c * SRC_STEPS)
                dve.wait_ge(s_x_in, 16 * c + 16)
                if not first:
                    dve.wait_ge(s_src, c * SRC_STEPS)
                    dve.wait_ge(s_h_out, 16 * c)
                    dve.wait_ge(s_src_t, c)
                layer_norm_stats(do, x_c[:, :], h_c[:, :], t_c[:, :])
                dve.wait_ge(s_src_pow, c + 1)
                do.did(v.scalar_tensor_tensor(out=tiles(h_c[:, :]), in0=tiles(h_c[:, :]), scalar=0.0,
                                              in1=per_node(rstd[:, :]), op0=ALU.max, op1=ALU.mult))
                assert do.n == SRC_STEPS

            over_chunks(dve, source)

            def add_window(it, n, g, rows, first, s_sum, sums, s_done):
                start = dve.value_load(base_i[0:1, bass.ds(it * GROUPS_PER_ITER + g, 1)], min_val=0, max_val=NODES)
                window = acc[0:rows, bass.ds(start, WINDOW)]
                if not first:
                    dve.wait_ge(s_done, GROUPS_PER_ITER * n + g)
                dve.wait_ge(s_sum, sums)
                v.tensor_tensor(window, window, sg[g][0:rows, 0:WINDOW], ALU.add).then_inc(s_done, 1)

            def move_windows(do):
                do.did(v.tensor_scalar(rel[:, :], rel[:, :], float(-WINDOW), None, ALU.add))
                do.did(v.tensor_scalar(base_f[:, :], base_f[:, :], float(WINDOW), float(N), ALU.add, ALU.min))
                do.wait()
                do.did(v.tensor_copy(base_i[:, :], base_f[0:1, :]))
                do.wait()

            def windows_back(s_back):
                with dve.Fori(0, rounds) as r:
                    v.tensor_scalar(rel[:, :], rel[:, :], float(WINDOW), None, ALU.add).then_inc(s_back, 1)
                    dve.wait_ge(s_back, r + 1)
                v.tensor_copy(base_f[:, :], first_base[:, :]).then_inc(s_window, 1)
                v.tensor_copy(base_i[:, :], first_base[0:1, :]).then_inc(s_window, 1)

            dve.wait_ge(s_ready, 1)
            rounds = load_rounds(dve)
            dve.wait_ge(s_acc0[0], 1)
            dve.wait_ge(s_src_ev, 4 * CHUNKS)

            def dst_quad(it, s):
                return rel[:, bass.ds(it * TILES_PER_ITER + QUAD * s, QUAD)].unsqueeze(2).to_broadcast([P, QUAD, WINDOW])

            def add(n, s):
                i = QUADS_PER_ITER * n + s
                dve.wait_ge(s_gath[s], QUAD * 16 * n + QUAD * 16)
                dve.wait_ge(s_attr_mm, i + 1)
                pair = hid[s][:, :, :].rearrange("p (b t) f -> p b (t f)", b=2)
                v.tensor_tensor(pair, attr_ps[s % 2][:, :].rearrange("p (b c) -> p b c", b=2)[:, :, 0:2 * H2], pair,
                                ALU.add).then_inc(s_added, 1)

            def dot(n, s, first):
                i = QUADS_PER_ITER * n + s
                dve.wait_ge(s_gelu, i + 1)
                if not first:
                    dve.wait_ge(s_dotted, i)
                v.tensor_tensor(prod[:, :, :], hid[s][:, :, D:H2],
                                gate_w2_ps.unsqueeze(1).to_broadcast([P, QUAD, D]), ALU.mult).then_inc(s_prod, 1)
                dve.wait_ge(s_prod, i + 1)
                v.tensor_reduce(logit[s % 2][:, :], prod[:, :, :], AX.X, ALU.add).then_inc(s_dotted, 1)

            def gate(it, n, s, free):
                i = QUADS_PER_ITER * n + s
                m = msg[s % 2]
                if free:
                    dve.wait_ge(s_seg, i - 1)
                v.tensor_tensor(hot[s % 2][:, :, :], iota.unsqueeze(1).to_broadcast([P, QUAD, WINDOW]),
                                dst_quad(it, s), ALU.is_equal)
                v.tensor_copy(m[:, :, DEG_ROW], weight[:, bass.ds(it * TILES_PER_ITER + QUAD * s, QUAD)])
                dve.wait_ge(s_tanh, i + 1)
                v.tensor_scalar(m[:, :, GATE_ROW], gate_t[s % 2][:, :], 0.5, 0.5, ALU.mult, ALU.add).then_inc(s_gcol, 1)
                dve.wait_ge(s_gcol, i + 1)
                v.tensor_tensor(m[:, :, 0:D], hid[s][:, :, 0:D],
                                m[:, :, GATE_ROW].unsqueeze(2).to_broadcast([P, QUAD, D]), ALU.mult).then_inc(s_gated, 1)

            def window_sum(it, n, g, first):
                add_window(it, n, g, ACC_ROWS, first, s_seg, QUADS_PER_ITER * n + 2 * g + 2, s_acc)

            def edges(it, n, first, last):
                if first:
                    add(n, 0)
                    add(n, 1)
                    dot(n, 0, True)
                for s in range(QUADS_PER_ITER):
                    if s + 2 < QUADS_PER_ITER:
                        add(n, s + 2)
                    elif not last:
                        add(n + 1, s + 2 - QUADS_PER_ITER)
                    if s + 1 < QUADS_PER_ITER:
                        dot(n, s + 1, False)
                    elif not last:
                        dot(n + 1, 0, False)
                    gate(it, n, s, not (first and s < 2))
                    if s == 0 and not first:
                        window_sum(it - 1, n - 1, 1, False)
                    if s == 2:
                        window_sum(it, n, 0, first)
                if last:
                    window_sum(it, n, 1, False)

            def round_end(r):
                dve.wait_ge(s_acc, r * GROUPS + GROUPS)
                move_windows(Steps(dve, s_shift, r * 3))

            edge_pass(dve, rounds, edges, round_end)
            windows_back(s_back[0])
            dve.wait_ge(s_window, 2)

            def update(c, first):
                do = Steps(dve, s_up, UPD_STEPS * c)
                if not first:
                    dve.wait_ge(s_up, UPD_STEPS * c)
                dve.wait_ge(s_up_in, 16 * c + 16)
                dve.wait_ge(s_up_mm, c + 1)
                for bank, k, m in NODE_SLOTS:
                    do.did(v.tensor_tensor(h_c[:, D * k:D * (k + m)], bank[:, 0:D * m], h_c[:, D * k:D * (k + m)], ALU.add))
                do.wait()
                layer_norm_stats(do, h_c[:, :], t_c[:, :], m_c[:, :])
                dve.wait_ge(s_up_pow, 3 * c + 1)
                do.did(v.tensor_tensor(tiles(t_c[:, :]), tiles(t_c[:, :]), per_node(rstd[:, :]), ALU.mult))
                do.wait()
                do.did(v.tensor_tensor(tiles(t_c[:, :]), tiles(t_c[:, :]), per_feature(ln_g[:, :]), ALU.mult))
                do.wait()
                do.did(v.tensor_tensor(tiles(t_c[:, :]), tiles(t_c[:, :]), per_feature(ln_b[:, :]), ALU.add))
                do.wait()
                dve.wait_ge(s_up_x, 16 * c + 16)
                do.did(v.tensor_tensor(x_c[:, :], x_c[:, :], t_c[:, :], ALU.add))
                do.wait()
                assert do.n == UPD_X1
                if not first:
                    dve.wait_ge(s_h1_out, 16 * c)
                layer_norm_stats(do, x_c[:, :], q_c[:, :], m_c[:, :])
                assert do.n == UPD_VAR2
                dve.wait_ge(s_up_pow, 3 * c + 2)
                do.did(v.scalar_tensor_tensor(out=tiles(q_c[:, :]), in0=tiles(q_c[:, :]), scalar=0.0,
                                              in1=per_node(rstd[:, :]), op0=ALU.max, op1=ALU.mult))
                do.did(v.tensor_scalar(st[:, 4, :], px[:, 0:TILES_PER_CHUNK], 1.0, None, ALU.add))
                do.wait()
                do.did(v.tensor_scalar(st[:, 5, :], st[:, 4, :], 0.0, None, ALU.is_gt))
                do.wait()
                do.did(v.tensor_tensor(st[:, 4, :], st[:, 4, :], st[:, 5, :], ALU.mult))
                do.did(v.tensor_scalar(st[:, 6, :], st[:, 5, :], -1.0, 1.0, ALU.mult, ALU.add))
                do.wait()
                do.did(v.tensor_tensor(st[:, 6, :], st[:, 6, :], st[:, 4, :], ALU.add))
                assert do.n == UPD_DEG
                dve.wait_ge(s_up_pow, 3 * c + 3)
                do.did(v.tensor_tensor(dinv[:, bass.ds(c * TILES_PER_CHUNK, TILES_PER_CHUNK)], rstd[:, :], st[:, 5, :],
                                       ALU.mult))
                assert do.n == UPD_STEPS

            over_chunks(dve, update)
            dve.wait_ge(s_up, UPD_STEPS * CHUNKS)

            for l in range(2):
                def project(c, first, s=pr[l]):
                    dve.wait_ge(s["mm"], c + 1)
                    if not first:
                        dve.wait_ge(s["table_out"], 16 * c)
                    for i, (bank, k, m) in enumerate(TABLE_SLOTS):
                        dve.wait_ge(s["tanh"], 4 * c + i + 1)
                        scale = dinv[:, bass.ds(c * TILES_PER_CHUNK + k, m)].unsqueeze(2).to_broadcast([P, m, D])
                        v.tensor_tensor(tiles(q_c[:, D * k:D * (k + m)]), tiles(bank, H2)[:, :, 0:D], scale,
                                        ALU.mult).then_inc(s["scaled"], 1)

                over_chunks(dve, project)

                dve.wait_ge(s_acc0[l + 1], 1)
                dve.wait_ge(pr[l]["tanh"], 4 * CHUNKS)

                def conv_edges(it, n, first, last, s=cv[l]):
                    for b in range(GROUPS_PER_ITER):
                        g = GROUPS_PER_ITER * n + b
                        cols = bass.ds(it * TILES_PER_ITER + GROUP * b, GROUP)
                        if not first:
                            dve.wait_ge(s["seg"], g - 1)
                        v.tensor_tensor(conv_s[b][:, :, :], iota.unsqueeze(1).to_broadcast([P, GROUP, WINDOW]),
                                        rel[:, cols].unsqueeze(2).to_broadcast([P, GROUP, WINDOW]),
                                        ALU.is_equal).then_inc(s["hot"], 1)
                        dve.wait_ge(s["hot"], g + 1)
                        v.tensor_tensor(conv_s[b][:, :, :], conv_s[b][:, :, :],
                                        weight[:, cols].unsqueeze(2).to_broadcast([P, GROUP, WINDOW]),
                                        ALU.mult).then_inc(s["weighted"], 1)
                        if b == 0 and not first:
                            conv_window(it - 1, n - 1, 1, False, s)
                        if b == 1:
                            conv_window(it, n, 0, first, s)
                    if last:
                        conv_window(it, n, 1, False, s)

                def conv_window(it, n, g, first, s):
                    add_window(it, n, g, D, first, s["seg"], GROUPS_PER_ITER * n + g + 1, s["acc"])

                def conv_end(r, s=cv[l]):
                    dve.wait_ge(s["acc"], r * GROUPS + GROUPS)
                    move_windows(Steps(dve, s["shift"], r * 3))

                edge_pass(dve, rounds, conv_edges, conv_end)
                windows_back(s_back[l + 1])
                dve.wait_ge(s_window, 2 * l + 4)

                def combine(c, first, s=cb[l], l=l):
                    do = Steps(dve, s["steps"], COMBINE_STEPS[l] * c)
                    t, h, m = tiles(t_c[:, :]), tiles(h_c[:, :]), tiles(m_c[:, :])
                    dve.wait_ge(s["q_in"], 16 * c + 16)
                    dve.wait_ge(s["t"], c + 1)
                    if not first:
                        dve.wait_ge(s["out"], 16 * c)
                    for bank, k, w in NODE_SLOTS:
                        do.did(v.tensor_tensor(t_c[:, D * k:D * (k + w)], bank[:, 0:D * w], q_c[:, D * k:D * (k + w)],
                                               ALU.add))
                    do.wait()
                    do.did(v.tensor_tensor(t, t, per_node(dinv[:, bass.ds(c * TILES_PER_CHUNK, TILES_PER_CHUNK)]), ALU.mult))
                    do.wait()
                    do.did(v.tensor_tensor(t, t, per_feature(conv_b[l][:, :]), ALU.add))
                    do.wait()
                    dve.wait_ge(s["h_in"], 16 * c + 16)
                    do.did(v.tensor_tensor(t, t, h, ALU.subtract))
                    do.wait()
                    dve.wait_ge(s["m_in"], 16 * c + 16)
                    do.did(v.tensor_tensor(t, t, m, ALU.mult))
                    do.wait()
                    do.did(v.tensor_tensor(t, t, h, ALU.add))
                    do.wait()
                    if l == 0:
                        do.did(v.tensor_scalar(t_c[:, :], t_c[:, :], 0.0, None, ALU.max))
                    else:
                        dve.wait_ge(s["x_in"], 16 * c + 16)
                        do.did(v.scalar_tensor_tensor(out=t_c[:, :], in0=t_c[:, :], scalar=0.0, in1=x_c[:, :],
                                                      op0=ALU.max, op1=ALU.add))
                    assert do.n == COMBINE_STEPS[l]

                over_chunks(dve, combine)


COMBINE_STEPS = [8, 8]


def kernel(x, src, dst, edge_attr_32, edge_weight, **w):
    import numpy as np
    import concourse.bacc as bacc
    from concourse.bass_utils import run_bass_kernel_spmd

    w = {k: np.asarray(v) for k, v in w.items()}
    g, c = (lambda n: w["L0_gnn_" + n]), (lambda n: w["L1_gnn_" + n])

    def padded(a, n, fill):
        a = np.asarray(a)
        out = np.full((n,) + a.shape[1:], fill, a.dtype)
        out[:len(a)] = a
        return out

    zeros = np.zeros((1, D), np.float32)
    row = lambda a: np.ascontiguousarray(a.reshape(1, -1))
    arrays = {
        "x": padded(x, NODES, 0).reshape(CHUNKS, P, CF),
        "src": padded(src, EDGES, 0).reshape(GROUPS, GROUP, P).transpose(0, 2, 1),
        "dst": padded(dst, EDGES, N).reshape(TILES, P).T,
        "weight": padded(edge_weight, EDGES, 0).reshape(TILES, P).T,
        "attr": padded(edge_attr_32, EDGES, 0).reshape(GROUPS, GROUP * P, ED).transpose(0, 2, 1),
        "w_src": np.concatenate([np.concatenate([g("mW1")[:D], g("gW1")[:D]], 1),
                                 np.concatenate([row(g("mb1")), row(g("gb1"))], 1)]),
        "w_attr": np.concatenate([g("mW1")[D:], g("gW1")[D:]], 1),
        "msg_w2_t": np.concatenate([g("mW2"), row(g("mb2"))]).T,
        "upd_top": g("uW1")[:D],
        "upd_bottom": g("uW1")[D:],
        "upd_b1": g("ub1").reshape(D, 1),
        "upd_w2": np.concatenate([g("uW2"), row(g("ub2"))]),
        "gate_w2": row(g("gW2")),
        "gate_b2": row(g("gb2")),
        "ln_g": row(g("ln_g")),
        "ln_b": row(g("ln_b")),
    }
    for l in range(2):
        arrays[f"conv_w{l}"] = np.concatenate([np.concatenate([c(f"W{l}"), c(f"Wr{l}")], 1),
                                               np.concatenate([zeros, row(c(f"br{l}"))], 1)])
        arrays[f"conv_b{l}"] = row(c(f"b{l}"))

    nc = bacc.Bacc("TRN2", target_bir_lowering=False, num_devices=1)
    in_map, io = {}, {}
    for name, a in arrays.items():
        a = np.ascontiguousarray(a)
        in_map["in_" + name] = a
        io[name] = nc.dram_tensor("in_" + name, a.shape, mybir.dt.from_np(a.dtype), kind="ExternalInput").ap()
    io["out"] = nc.dram_tensor("out_nodes", [CHUNKS, P, CF], F32, kind="ExternalOutput").ap()
    build(nc, io)
    r = run_bass_kernel_spmd(nc, [in_map], core_ids=[0])
    return r.results[0]["out_nodes"].reshape(NODES, D)[:N]
```

```python
import contextlib

import concourse.bass as bass
import concourse.mybir as mybir
from concourse.alu_op_type import AluOpType as ALU

F32 = mybir.dt.float32
I32 = mybir.dt.int32
ACT = mybir.ActivationFunctionType
AX = mybir.AxisListType

N = 12500
E = 400000
D = 96
ED = 32
P = 128
EPS = 1e-5

TILES_PER_CHUNK = 7
CHUNK = P * TILES_PER_CHUNK
CHUNKS = -(-N // CHUNK)
NODES = CHUNKS * CHUNK
CF = TILES_PER_CHUNK * D

QUAD = 4
GROUP = 8
QUADS_PER_ITER = 4
GROUPS_PER_ITER = 2
TILES_PER_ITER = QUAD * QUADS_PER_ITER
ITERS = -(-E // (P * TILES_PER_ITER))
QUADS = ITERS * QUADS_PER_ITER
GROUPS = ITERS * GROUPS_PER_ITER
TILES = ITERS * TILES_PER_ITER
EDGES = TILES * P
WINDOW = 64
WINDOW_LOG2 = 6
ACC = NODES + WINDOW
GATE_ROW = D
DEG_ROW = D + 1
ACC_ROWS = D + 2
H2 = 2 * D
GB = GROUPS // 4
WEIGHT_LOADS = 18
SETUP_STEPS = 22
POOL_CONSTANTS = 9
MIX_STEPS = 6
MIX_SPAN = (ITERS - 2) // CHUNKS
HALF = CHUNK // 2
UPD_ROWS = D + 3


def after(engine, semaphore, value):
    if not (isinstance(value, int) and value <= 0):
        engine.wait_ge(semaphore, value)


class Steps:

    def __init__(self, engine, semaphore, base):
        self.engine, self.semaphore, self.base, self.n = engine, semaphore, base, 0

    def did(self, instruction):
        self.n += 1
        return instruction.then_inc(self.semaphore, 1)

    def wait(self):
        self.engine.wait_ge(self.semaphore, self.base + self.n)


LN_STATS = 6
SRC_STEPS = 7
UPD_READ = 4
UPD_VAR1 = UPD_READ + LN_STATS
UPD_DEG = UPD_VAR1 + 4
UPD_X1 = UPD_DEG + 4
UPD_VAR2 = UPD_X1 + LN_STATS
UPD_H1 = UPD_VAR2 + 1
UPD_STEPS = UPD_H1 + 1
COMB_READ = 1
COMB_STEPS = [3, 2]


def build(nc, io):
    ctx = contextlib.ExitStack()
    with ctx:
        def sb(name, shape, dt=F32):
            return ctx.enter_context(nc.sbuf_tensor(name, shape, dt))

        def ps(name, columns):
            return ctx.enter_context(nc.psum_tensor(name, [P, columns], F32))

        def sem(name):
            return ctx.enter_context(nc.semaphore(name))

        def dram(name, shape):
            return nc.dram_tensor(name, shape, F32).ap()

        src_table = dram("src_table", [CHUNKS, P, TILES_PER_CHUNK * H2])
        conv_table = [dram(f"conv_table{l}", [CHUNKS, P, CF]) for l in range(2)]
        h_src = dram("h_src", [CHUNKS, P, CF])
        x1_keep = dram("x1_keep", [CHUNKS, P, CF])
        dinv_rows = dram("dinv_rows", [CHUNKS, P, TILES_PER_CHUNK])
        mix_scale = [dram(f"mix_scale{l}", [CHUNKS, D, CHUNK]) for l in range(2)]
        mix_add = [dram(f"mix_add{l}", [CHUNKS, D, CHUNK]) for l in range(2)]
        src_rows = src_table.rearrange("c p (k f) -> (c p k) f", f=H2)
        conv_rows = [t.rearrange("c p (k f) -> (c p k) f", f=D) for t in conv_table]

        acc = sb("acc", [P, ACC])
        feat = sb("feat", [P, NODES])
        rel = sb("rel", [P, TILES])
        weight = sb("weight", [P, TILES])
        base_f = sb("base_f", [P, GROUPS])
        base_i = sb("base_i", [1, GROUPS], I32)
        first_base = sb("first_base", [P, GROUPS])
        rounds_i = sb("rounds_i", [1, 1], I32)
        dinv = sb("dinv", [P, CHUNKS * TILES_PER_CHUNK])
        ident = sb("ident", [P, P])
        ones = sb("ones", [P, P])
        zero = sb("zero", [P, 1])
        w_src = sb("w_src", [D + 1, H2])
        w_attr = sb("w_attr", [ED, H2])
        gate_w2 = sb("gate_w2", [P, D])
        gate_b2 = sb("gate_b2", [P, 1])
        gate_b2_half = sb("gate_b2_half", [P, 1])
        msg_w2_t = sb("msg_w2_t", [D, D + 1])
        upd_top = sb("upd_top", [D, D])
        upd_bottom = sb("upd_bottom", [D, D])
        msg_upd = sb("msg_upd", [D + 1, D])
        upd_b1 = sb("upd_b1", [D, 1])
        upd_w2 = sb("upd_w2", [UPD_ROWS, D + 1])
        ln_g = sb("ln_g", [P, D])
        ln_b = sb("ln_b", [P, D])
        conv_w = [sb(f"conv_w{l}", [D, H2]) for l in range(2)]
        conv_b = [sb(f"conv_b{l}", [D, 1]) for l in range(2)]
        mix_b = [sb(f"mix_b{l}", [D, 1]) for l in range(2)]
        mix_b_half = [sb(f"mix_b_half{l}", [D, 1]) for l in range(2)]
        act_warm = sb("act_warm", [P, 1])

        x_c = [sb(f"x_c{p}", [P, CF]) for p in range(2)]
        buf_h = [sb(f"buf_h{p}", [P, CHUNK]) for p in range(2)]
        buf_b = [sb(f"buf_b{p}", [P, CHUNK]) for p in range(2)]
        t_c = sb("t_c", [P, CHUNK])
        m_c = sb("m_c", [P, CF])
        s_c = sb("s_c", [P, TILES_PER_CHUNK * H2])
        h_t = [sb(f"h_t{p}", [D + 1, CHUNK]) for p in range(2)]
        st = sb("st", [P, 8, TILES_PER_CHUNK])
        rstd = sb("rstd", [P, 2, TILES_PER_CHUNK])
        neg_half = sb("neg_half", [P, 2, TILES_PER_CHUNK])
        h_c = [b[:, 0:CF] for b in buf_h]
        q_c = buf_b[1][:, 0:CF]
        u_t = buf_b[0][0:UPD_ROWS, :]
        scale_c = [b[0:D, :] for b in buf_h]
        add_c = [b[0:D, :] for b in buf_b]
        dinv_c, mix_c = scale_c[1], add_c[1]
        tab_c = s_c[:, 0:CF]
        src_ids = [sb(f"src_ids{b}", [P, GROUP], I32) for b in range(GROUPS_PER_ITER)]
        attr = [sb(f"attr{b}", [ED, GROUP * P]) for b in range(GROUPS_PER_ITER)]
        hid = [sb(f"hid{s}", [P, QUAD, H2]) for s in range(QUADS_PER_ITER)]
        prod = sb("prod", [P, QUAD, D])
        logit = [sb(f"logit{b}", [P, QUAD]) for b in range(2)]
        gate_t = [sb(f"gate_t{b}", [P, QUAD]) for b in range(2)]
        msg = [sb(f"msg{b}", [P, QUAD, ACC_ROWS]) for b in range(2)]
        hot = [sb(f"hot{b}", [P, QUAD, WINDOW]) for b in range(2)]
        hid_flat = [h[:, :, :].rearrange("p t f -> p (t f)") for h in hid]
        conv_g = [h.rearrange("p (t f) -> p t f", f=D) for h in hid_flat[0:2]]
        conv_s = [h[:, 0:GROUP * WINDOW].rearrange("p (t f) -> p t f", f=WINDOW) for h in hid_flat[2:4]]
        dst_f = feat[:, 0:TILES]
        dst_i = dst_f.bitcast(I32)
        lim = feat[:, TILES:TILES + 2 * GROUPS].rearrange("p (m g) -> p m g", m=2)
        iota_i = sb("iota_i", [P, WINDOW], I32)
        lim_g = sb("lim_g", [GB, 8, 4])
        diag = sb("diag", [GB, 4, GB])
        span = sb("span", [GB, 2])
        top = sb("top", [1, 2])
        top_i = sb("top_i", [1, 2], I32)

        pa = ps("pa", 1024)
        pb = ps("pb", 1024)
        sg = [ps("sg0", 512), ps("sg1", 512)]
        px = ps("px", 512)
        const = ps("const", 512)
        iota = const[:, 0:WINDOW]
        gate_w2_ps = const[:, WINDOW:WINDOW + D]
        attr_ps = [pa, pb]
        table_ps = [px[:, 0:4 * D], const[:, WINDOW + D:WINDOW + 4 * D]]

        s_weights = sem("weights_in")
        s_edges = sem("edges_in")
        s_pool_const = sem("pool_const")
        s_setup = sem("setup_steps")
        s_setup_pe = sem("setup_pe")
        s_ready = sem("setup_ready")
        s_bias = sem("bias_ready")
        s_x_in = [sem(f"x_in{p}") for p in range(2)]
        s_src = sem("src_steps")
        s_src_pow = sem("src_pow")
        s_src_t = sem("src_transposed")
        s_src_ht = sem("src_ht")
        s_src_mm = sem("src_product")
        s_src_ev = sem("src_copied")
        s_h_out = [sem(f"h_out{p}") for p in range(2)]
        s_table_out = sem("table_out")
        s_ids = [sem(f"ids_in{b}") for b in range(GROUPS_PER_ITER)]
        s_attr = [sem(f"attr_in{b}") for b in range(GROUPS_PER_ITER)]
        s_gath = [sem(f"gathered{s}") for s in range(QUADS_PER_ITER)]
        s_attr_mm = sem("attr_product")
        s_added = sem("added")
        s_gelu = sem("gelu_done")
        s_prod = sem("gate_products")
        s_dotted = sem("gate_logits")
        s_tanh = sem("tanh_done")
        s_gcol = sem("gate_columns")
        s_gated = sem("gated")
        s_seg = sem("segment_sums")
        s_acc = sem("accumulated")
        s_shift = sem("windows_moved")
        s_back = [sem(f"rel_back{p}") for p in range(3)]
        s_window = sem("windows_back")
        s_passed = sem("passed")
        s_acc0 = [sem(f"acc_zeroed{p}") for p in range(3)]
        s_up_in = [sem(f"upd_in{p}") for p in range(2)]
        s_up_u = sem("upd_hidden")
        s_up_g = sem("upd_gelu")
        s_up_mm = sem("upd_product")
        s_up = sem("upd_steps")
        s_up_pow = sem("upd_pow")
        s_up_t = sem("upd_transposed")
        s_up_ht = sem("upd_ht")
        s_x1_out = sem("x1_out")
        s_dinv_out = sem("dinv_out")
        tb = [{k: sem(f"table{l}_{k}") for k in ("mm", "scaled", "out")} for l in range(2)]
        cv = [{k: sem(f"conv{l}_{k}") for k in
               ("ids0", "ids1", "gath0", "gath1", "hot", "weighted", "seg", "acc", "shift")} for l in range(2)]
        mx = [{k: sem(f"mix{l}_{k}") for k in
               ("dinv_in", "products", "tanh", "steps", "done", "out")} for l in range(2)]
        cb = [{k: sem(f"comb{l}_{k}") for k in ("in0", "in1", "steps", "kept")} for l in range(2)]
        s_x1_in = [sem(f"x1_in{p}") for p in range(2)]
        s_out_t = sem("out_transposed")
        s_final = sem("out_steps")
        s_out = sem("out_stored")

        block = ctx.enter_context(nc.Block())

        def tiles(ap, f=D):
            return ap.rearrange("p (k f) -> p k f", f=f)

        def per_node(ap):
            return ap.unsqueeze(2).to_broadcast([P, TILES_PER_CHUNK, D])

        def per_feature(ap, k=TILES_PER_CHUNK):
            return ap.unsqueeze(1).to_broadcast([P, k, D])

        def chunk(t, c):
            return t[bass.ds(c, 1), :, :].rearrange("o p f -> (o p) f")

        def columns(t, c, rows):
            return t[0:rows, bass.ds(c * CHUNK, CHUNK)]

        def half_columns(t, c, i, rows):
            return t[0:rows, bass.ds(c * CHUNK + i * HALF, HALF)]

        def by_tile(ap):
            return ap.rearrange("r (p k) -> r k p", k=TILES_PER_CHUNK)

        def tile_cols(t, k, rows):
            return t[0:rows, k * P:(k + 1) * P]

        def node_cols(t, k, rows):
            return by_tile(t[0:rows, :])[:, k, :]

        def halves(ap):
            return ap[0:D, :].rearrange("r (b n) -> r b n", b=2)[:, :, 0:HALF]

        def split(ap):
            return ap.rearrange("r (b n) -> r b n", b=2)

        def table_slot(k):
            if k < 4:
                return pb[:, 512 * (k // 2) + H2 * (k % 2):512 * (k // 2) + H2 * (k % 2 + 1)]
            return sg[(k - 4) // 2][:, H2 * (k % 2):H2 * (k % 2 + 1)]

        TABLE_SLOTS = [(pb[:, 0:2 * H2], 0, 2), (pb[:, 512:512 + 2 * H2], 2, 2),
                       (sg[0][:, 0:2 * H2], 4, 2), (sg[1][:, 0:H2], 6, 1)]
        NODE_SLOTS = [(0, 4), (4, 3)]

        def node_slot(banks, k, f=D):
            return banks[k // 4][:, f * (k % 4):f * (k % 4 + 1)]

        def over_chunks(eng, body):
            for c in (0, 1):
                body(c, c, 0)
            with eng.Fori(1, CHUNKS // 2 - 1) as pair:
                c = eng.snap(pair * 2)
                body(c, 0, pair)
                body(c + 1, 1, pair)
            for c in (CHUNKS - 2, CHUNKS - 1):
                body(c, c % 2, c // 2)

        def is_at(c, *chunks):
            return isinstance(c, int) and c in chunks

        def wait_apart(eng, semaphore, value):
            eng.wait_ge(semaphore, value)
            if not isinstance(value, int):
                eng.sem_inc(s_passed, 1)

        def load_rounds(eng):
            return eng.value_load(rounds_i[0:1, 0:1], min_val=1, max_val=N // WINDOW + 1)

        def edge_pass(eng, rounds, iteration, round_end, mix=None):
            with eng.Fori(0, rounds) as r:
                n0 = eng.snap(r * ITERS)
                iteration(0, n0, True, False)
                if mix:
                    start, middle, end = mix
                    with eng.Fori(0, CHUNKS) as c:
                        done = eng.snap(r * CHUNKS + c)
                        i0 = eng.snap(c * MIX_SPAN + 1)
                        if start:
                            start(c, done)
                        with eng.Fori(0, MIX_SPAN // 2) as j:
                            iteration(i0 + j, n0 + i0 + j, False, False)
                        if middle:
                            middle(c, done)
                        with eng.Fori(MIX_SPAN // 2, MIX_SPAN) as j:
                            iteration(i0 + j, n0 + i0 + j, False, False)
                        if end:
                            end(c, done)
                with eng.Fori(CHUNKS * MIX_SPAN + 1 if mix else 1, ITERS - 1) as it:
                    iteration(it, n0 + it, False, False)
                iteration(ITERS - 1, n0 + (ITERS - 1), False, True)
                round_end(r)

        def transposes(src):
            for k in range(TILES_PER_CHUNK):
                last = nc.tensor.transpose(pa[0:D, 512 * (k // 4) + P * (k % 4):512 * (k // 4) + P * (k % 4 + 1)],
                                           src[:, k * D:(k + 1) * D], ident[:, :])
            return last

        @block.sync
        def _(sp):
            sp.dma_start(dst_i, io["dst"]).then_inc(s_edges, 16)
            for p in range(2):
                sp.dma_start(x_c[p][:, :], chunk(io["x"], p)).then_inc(s_x_in[p], 16)
            for name, t in (("w_src", w_src), ("w_attr", w_attr), ("msg_w2_t", msg_w2_t), ("upd_top", upd_top),
                            ("upd_bottom", upd_bottom), ("upd_b1", upd_b1), ("upd_w2", upd_w2),
                            ("conv_w0", conv_w[0]), ("conv_w1", conv_w[1]), ("conv_b0", conv_b[0]),
                            ("conv_b1", conv_b[1]), ("mix_b0", mix_b[0]), ("mix_b1", mix_b[1])):
                sp.dma_start(t[:, :], io[name]).then_inc(s_weights, 16)
            for name, t in (("gate_w2", gate_w2), ("gate_b2", gate_b2), ("ln_g", ln_g), ("ln_b", ln_b)):
                sp.dma_start(t[:, :], io[name].partition_broadcast(P)).then_inc(s_weights, 16)
            sp.dma_start(weight[:, :], io["weight"]).then_inc(s_weights, 16)

            def table(c):
                sp.wait_ge(s_src_ev, 4 * c + 4)
                sp.dma_start(chunk(src_table, c), s_c[:, :]).then_inc(s_table_out, 16)

            def source(c, p, pair):
                sp.wait_ge(s_src, SRC_STEPS * c + SRC_STEPS)
                sp.dma_start(chunk(h_src, c), h_c[p]).then_inc(s_h_out[p], 16)
                if not is_at(c, CHUNKS - 2, CHUNKS - 1):
                    sp.dma_start(x_c[p][:, :], chunk(io["x"], c + 2)).then_inc(s_x_in[p], 16)
                if not is_at(c, 0):
                    table(c - 1)

            over_chunks(sp, source)
            table(CHUNKS - 1)

            sp.wait_ge(s_ready, 1)
            rounds = load_rounds(sp)

            def edges(it, n, first, last):
                for b in range(GROUPS_PER_ITER):
                    if not first:
                        sp.wait_ge(s_gath[2 * b], QUAD * 16 * n)
                        sp.wait_ge(s_gath[2 * b + 1], QUAD * 16 * n)
                    sp.dma_start(src_ids[b][:, :], chunk(io["src"], it * 2 + b)).then_inc(s_ids[b], 16)
                    if not first:
                        sp.wait_ge(s_attr_mm, QUADS_PER_ITER * (n - 1) + 2 * b + 2)
                    sp.dma_start(attr[b][:, :], chunk(io["attr"], it * 2 + b)).then_inc(s_attr[b], 16)

            edge_pass(sp, rounds, edges, lambda r: wait_apart(sp, s_acc, r * GROUPS + GROUPS))

            for p in range(2):
                sp.wait_ge(s_h_out[p], 16 * (CHUNKS // 2))

            def load_update(c, p):
                sp.dma_start(h_c[p], chunk(h_src, c)).then_inc(s_up_in[p], 16)
                sp.dma_start(x_c[p][:, :], chunk(io["x"], c)).then_inc(s_up_in[p], 16)

            def store_table(c, l):
                sp.wait_ge(tb[l]["scaled"], 2 * c + 2)
                sp.dma_start(chunk(conv_table[l], c), tab_c).then_inc(tb[l]["out"], 16)

            def update(c, p, pair):
                sp.wait_ge(s_up, UPD_STEPS * c + UPD_X1)
                sp.dma_start(chunk(x1_keep, c), x_c[p][:, :]).then_inc(s_x1_out, 16)
                if not is_at(c, CHUNKS - 2, CHUNKS - 1):
                    sp.wait_ge(s_up, UPD_STEPS * c + UPD_VAR2)
                    sp.wait_ge(s_x1_out, 16 * c + 16)
                    load_update(c + 2, p)
                if not is_at(c, 0):
                    store_table(c - 1, 0)

            for p in range(2):
                load_update(p, p)
            over_chunks(sp, update)
            sp.wait_ge(s_up, UPD_STEPS * CHUNKS)
            sp.dma_start(dinv_rows.rearrange("c p k -> p c k"),
                         dinv[:, :].rearrange("p (c k) -> p c k", k=TILES_PER_CHUNK)).then_inc(s_dinv_out, 16)
            store_table(CHUNKS - 1, 0)
            sp.wait_ge(s_x1_out, 16 * CHUNKS)
            sp.wait_ge(s_dinv_out, 16)

            for l in range(2):
                def conv_edges(it, n, first, last, s=cv[l]):
                    for b in range(GROUPS_PER_ITER):
                        if not first:
                            sp.wait_ge(s[f"gath{b}"], GROUP * 16 * n)
                        sp.dma_start(src_ids[b][:, :], chunk(io["src"], it * 2 + b)).then_inc(s[f"ids{b}"], 16)

                def load_dinv(c, done, s=mx[l]):
                    wait_apart(sp, s["done"], done + 1)
                    row = dinv_rows[bass.ds(c, 1), :, :].rearrange("o p k -> o (p k)")
                    sp.dma_start(dinv_c, row.partition_broadcast(D)).then_inc(s["dinv_in"], 16)

                def store_mix(c, done, s=mx[l], l=l):
                    wait_apart(sp, s["done"], done + 2)
                    sp.dma_start(chunk(mix_scale[l], c), scale_c[0]).then_inc(s["out"], 16)
                    sp.dma_start(chunk(mix_add[l], c), add_c[0]).then_inc(s["out"], 16)

                def conv_end(r, l=l):
                    wait_apart(sp, cv[l]["acc"], r * GROUPS + GROUPS)
                    wait_apart(sp, mx[l]["out"], r * (32 * CHUNKS) + (32 * CHUNKS + 32))

                sp.sem_inc(mx[l]["done"], 1)
                sp.sem_inc(mx[l]["out"], 32)
                edge_pass(sp, rounds, conv_edges, conv_end, mix=(load_dinv, None, store_mix))

                def load_mix(c, p, s=cb[l], l=l):
                    sp.dma_start(scale_c[p], chunk(mix_scale[l], c)).then_inc(s[f"in{p}"], 16)
                    sp.dma_start(add_c[p], chunk(mix_add[l], c)).then_inc(s[f"in{p}"], 16)

                def store_out(c):
                    sp.wait_ge(s_final, 2 * c + 2)
                    sp.dma_start(chunk(io["out"], c), tab_c).then_inc(s_out, 16)

                def load_x1(c, p):
                    sp.dma_start(x_c[p][:, :], chunk(x1_keep, c)).then_inc(s_x1_in[p], 16)

                def combine(c, p, pair, l=l):
                    sp.wait_ge(cb[l]["steps"], COMB_STEPS[l] * c + COMB_STEPS[l])
                    if not is_at(c, CHUNKS - 2, CHUNKS - 1):
                        load_mix(c + 2, p)
                    if not is_at(c, 0):
                        if l == 0:
                            store_table(c - 1, 1)
                        else:
                            store_out(c - 1)
                            if not is_at(c, CHUNKS - 1):
                                load_x1(c + 1, 1 - p)

                for p in range(2):
                    load_mix(p, p)
                    if l == 1:
                        load_x1(p, p)
                over_chunks(sp, combine)
                if l == 0:
                    store_table(CHUNKS - 1, 1)
                else:
                    store_out(CHUNKS - 1)
            sp.wait_ge(s_out, 16 * CHUNKS)

        @block.gpsimd
        def _(pool):
            do = Steps(pool, s_pool_const, 0)
            for fill in (lambda: pool.memset(ident[:, :], 0.0),
                         lambda: pool.affine_select(out=ident[:, :], in_=ident[:, :], compare_op=ALU.not_equal,
                                                    fill=1.0, base=0, pattern=[[-1, P]], channel_multiplier=1),
                         lambda: pool.memset(ones[:, :], 1.0),
                         lambda: pool.iota(iota_i[:, :], pattern=[[1, WINDOW]], base=0, channel_multiplier=0),
                         lambda: pool.memset(h_t[0][D:D + 1, :], 1.0),
                         lambda: pool.memset(h_t[1][D:D + 1, :], 1.0),
                         lambda: pool.memset(u_t[D:UPD_ROWS, :], 1.0),
                         lambda: pool.memset(zero[:, :], 0.0),
                         lambda: pool.memset(neg_half[:, :, :], -0.5)):
                do.did(fill())
                do.wait()
            pool.memset(acc[:, :], 0.0).then_inc(s_acc0[0], 1)
            pool.wait_ge(s_acc0[0], 1)

            with pool.Fori(0, CHUNKS) as c:
                pool.wait_ge(s_src, c * SRC_STEPS + LN_STATS)
                pool.tensor_tensor(rstd[:, 0, :], st[:, 3, :], neg_half[:, 0, :], ALU.pow).then_inc(s_src_pow, 1)

            pool.wait_ge(s_ready, 1)
            rounds = load_rounds(pool)
            pool.wait_ge(s_table_out, 16 * CHUNKS)

            def gather(it, n, first, last):
                for s in range(QUADS_PER_ITER):
                    if s % 2 == 0:
                        wait_apart(pool, s_ids[s // 2], 16 * n + 16)
                    if not first:
                        wait_apart(pool, s_gated, QUADS_PER_ITER * (n - 1) + s + 1)
                    for t in range(QUAD):
                        j = QUAD * (s % 2) + t
                        pool.indirect_dma_start(
                            out=hid[s][:, t, :], out_offset=None, in_=src_rows,
                            in_offset=bass.IndirectOffsetOnAxis(ap=src_ids[s // 2][:, j:j + 1], axis=0),
                        ).then_inc(s_gath[s], 16)

            edge_pass(pool, rounds, gather, lambda r: wait_apart(pool, s_acc, r * GROUPS + GROUPS))

            with pool.Fori(0, CHUNKS) as c:
                pool.wait_ge(s_up, UPD_STEPS * c + UPD_VAR1)
                pool.tensor_tensor(rstd[:, 0, :], st[:, 3, :], neg_half[:, 0, :], ALU.pow).then_inc(s_up_pow, 1)
                pool.wait_ge(s_up_u, c + 1)
                pool.tensor_copy(columns(acc, c, D), zero[0:D, :].to_broadcast([D, CHUNK])).then_inc(s_acc0[1], 1)
                pool.wait_ge(s_up, UPD_STEPS * c + UPD_VAR2)
                pool.tensor_tensor(rstd[:, :, :], st[:, 3:5, :], neg_half[:, :, :], ALU.pow).then_inc(s_up_pow, 1)

            for l in range(2):
                pool.wait_ge(tb[l]["out"], 16 * CHUNKS)

                def conv_gather(it, n, first, last, s=cv[l], l=l):
                    for b in range(GROUPS_PER_ITER):
                        wait_apart(pool, s[f"ids{b}"], 16 * n + 16)
                        if not first:
                            wait_apart(pool, s["seg"], GROUPS_PER_ITER * (n - 1) + b + 1)
                        for t in range(GROUP):
                            pool.indirect_dma_start(
                                out=conv_g[b][:, t, :], out_offset=None, in_=conv_rows[l],
                                in_offset=bass.IndirectOffsetOnAxis(ap=src_ids[b][:, t:t + 1], axis=0),
                            ).then_inc(s[f"gath{b}"], 16)

                edge_pass(pool, rounds, conv_gather,
                          lambda r, s=cv[l]: wait_apart(pool, s["acc"], r * GROUPS + GROUPS))

                if l == 0:
                    with pool.Fori(0, CHUNKS) as c:
                        pool.wait_ge(cb[0]["steps"], COMB_STEPS[0] * c + COMB_READ)
                        pool.tensor_copy(columns(acc, c, D), zero[0:D, :].to_broadcast([D, CHUNK])).then_inc(s_acc0[2], 1)

        @block.tensor
        def _(pe):
            pe.wait_ge(s_pool_const, POOL_CONSTANTS)
            pe.wait_ge(s_weights, 16 * WEIGHT_LOADS)
            nc.tensor.matmul(px[0:D + 1, 400:400 + D], msg_w2_t[:, :], upd_bottom[:, :],
                             start=True, stop=True).then_inc(s_setup_pe, 1)
            pe.wait_ge(s_setup, 4)
            for m, bank in ((0, pa), (1, pb)):
                for q in range(4):
                    last = nc.tensor.transpose(bank[0:GB, P * q:P * (q + 1)],
                                               lim[:, m, GB * q:GB * (q + 1)], ident[:, :])
            last.then_inc(s_setup_pe, 1)
            pe.wait_ge(s_setup, 12)
            nc.tensor.matmul(sg[0][0:1, 0:GB], span[:, 0:1], ident[0:GB, 0:GB], start=True, stop=True)
            for q in range(4):
                last = nc.tensor.matmul(sg[1][:, GB * q:GB * (q + 1)], ones[0:GB, :], diag[:, q, :],
                                        start=True, stop=True)
            last.then_inc(s_setup_pe, 1)

            pe.wait_ge(s_ready, 1)

            def products(c, p):
                pe.wait_ge(s_src_ht, 4 * c + 2)
                after(pe, s_src_ev, 4 * c)
                for k in range(TILES_PER_CHUNK):
                    last = nc.tensor.matmul(table_slot(k), tile_cols(h_t[p], k, D + 1), w_src[:, :],
                                            start=True, stop=True)
                last.then_inc(s_src_mm, 1)

            def source(c, p, pair):
                pe.wait_ge(s_src, c * SRC_STEPS + SRC_STEPS)
                after(pe, s_src_ht, 4 * c)
                transposes(h_c[p]).then_inc(s_src_t, 1)
                if not is_at(c, 0):
                    products(c - 1, 1 - p)

            over_chunks(pe, source)
            products(CHUNKS - 1, (CHUNKS - 1) % 2)

            rounds = load_rounds(pe)
            pe.wait_ge(s_src_ev, 4 * CHUNKS)

            def attr_product(n, s, free):
                if s % 2 == 0:
                    pe.wait_ge(s_attr[s // 2], 16 * n + 16)
                if free:
                    pe.wait_ge(s_added, QUADS_PER_ITER * n + s - 1)
                for t in range(QUAD):
                    col = P * (QUAD * (s % 2) + t)
                    last = nc.tensor.matmul(
                        attr_ps[s % 2][:, 512 * (t // 2) + H2 * (t % 2):512 * (t // 2) + H2 * (t % 2 + 1)],
                        attr[s // 2][:, col:col + P], w_attr[:, :], start=True, stop=True)
                last.then_inc(s_attr_mm, 1)

            def edges(it, n, first, last):
                if first:
                    for s in range(3):
                        attr_product(n, s, s == 2)
                for s in range(QUADS_PER_ITER):
                    if s + 3 < QUADS_PER_ITER:
                        attr_product(n, s + 3, True)
                    elif not last:
                        attr_product(n + 1, s + 3 - QUADS_PER_ITER, True)
                    pe.wait_ge(s_gated, QUADS_PER_ITER * n + s + 1)
                    if s % 2 == 0 and not first:
                        pe.wait_ge(s_acc, GROUPS_PER_ITER * (n - 1) + s // 2 + 1)
                    for t in range(QUAD):
                        op = nc.tensor.matmul(sg[s // 2][0:ACC_ROWS, 0:WINDOW], msg[s % 2][:, t, :],
                                              hot[s % 2][:, t, :], start=(s % 2 == 0 and t == 0),
                                              stop=(s % 2 == 1 and t == QUAD - 1))
                    op.then_inc(s_seg, 1)

            edge_pass(pe, rounds, edges, lambda r: pe.wait_ge(s_acc, r * GROUPS + GROUPS))

            def hidden(c):
                for i in range(2):
                    out = pb[0:D, 512 * i:512 * i + HALF]
                    nc.tensor.matmul(out, upd_top[:, :], half_columns(feat, c, i, D), start=True, stop=False)
                    last = nc.tensor.matmul(out, msg_upd[:, :], half_columns(acc, c, i, D + 1), start=False, stop=True)
                last.then_inc(s_up_u, 1)

            def new_h(c):
                pe.wait_ge(s_up, UPD_STEPS * c + UPD_STEPS)
                after(pe, s_up_ht, 4 * c)
                transposes(q_c).then_inc(s_up_t, 1)

            def table_rows(c, p, l):
                after(pe, tb[l]["scaled"], 2 * c)
                for k in range(TILES_PER_CHUNK):
                    nodes = tile_cols(h_t[p], k, D) if l == 0 else node_cols(h_t[p], k, D)
                    last = nc.tensor.matmul(node_slot(table_ps, k), nodes, conv_w[l][:, 0:D], start=True, stop=True)
                last.then_inc(tb[l]["mm"], 1)

            def update(c, p, pair):
                pe.wait_ge(s_up_g, 3 * c + 3)
                if not is_at(c, 0):
                    pe.wait_ge(s_up, UPD_STEPS * (c - 1) + UPD_READ)
                for k in range(TILES_PER_CHUNK):
                    last = nc.tensor.matmul(node_slot(sg, k, D + 1), node_cols(u_t, k, UPD_ROWS), upd_w2[:, :],
                                            start=True, stop=True)
                last.then_inc(s_up_mm, 1)
                if not is_at(c, CHUNKS - 1):
                    hidden(c + 1)
                if not is_at(c, 0):
                    new_h(c - 1)
                    pe.wait_ge(s_up_ht, 4 * (c - 1) + 2)
                    table_rows(c - 1, 1 - p, 0)

            hidden(0)
            over_chunks(pe, update)
            new_h(CHUNKS - 1)
            pe.wait_ge(s_up_ht, 4 * (CHUNKS - 1) + 2)
            table_rows(CHUNKS - 1, (CHUNKS - 1) % 2, 0)

            for l in range(2):
                if l == 0:
                    pe.wait_ge(s_up_ht, 4 * CHUNKS)
                else:
                    pe.wait_ge(cb[0]["kept"], CHUNKS)

                def conv_edges(it, n, first, last, s=cv[l]):
                    for b in range(GROUPS_PER_ITER):
                        pe.wait_ge(s[f"gath{b}"], GROUP * 16 * n + GROUP * 16)
                        pe.wait_ge(s["weighted"], GROUPS_PER_ITER * n + b + 1)
                        if not first:
                            pe.wait_ge(s["acc"], GROUPS_PER_ITER * (n - 1) + b + 1)
                        for t in range(GROUP):
                            op = nc.tensor.matmul(sg[b][0:D, 0:WINDOW], conv_g[b][:, t, :], conv_s[b][:, t, :],
                                                  start=(t == 0), stop=(t == GROUP - 1))
                        op.then_inc(s["seg"], 1)

                def mix_products(c, done, l=l):
                    wait_apart(pe, mx[l]["done"], done + 1)
                    for bank, w in ((pa, conv_w[l][:, D:H2]), (pb, conv_w[l][:, 0:D])):
                        for i in range(2):
                            last = nc.tensor.matmul(bank[0:D, 512 * i:512 * i + HALF], w, half_columns(feat, c, i, D),
                                                    start=True, stop=True)
                    last.then_inc(mx[l]["products"], 1)

                edge_pass(pe, rounds, conv_edges, lambda r, s=cv[l]: pe.wait_ge(s["acc"], r * GROUPS + GROUPS),
                          mix=(None, mix_products, None))

                def combine(c, p, pair, l=l):
                    pe.wait_ge(cb[l]["steps"], COMB_STEPS[l] * c + COMB_STEPS[l])
                    if l == 0:
                        table_rows(c, p, 1)
                    else:
                        after(pe, s_final, 2 * c)
                        for k in range(TILES_PER_CHUNK):
                            last = nc.tensor.transpose(node_slot(sg, k), node_cols(h_t[p], k, D), ident[0:D, 0:D])
                        last.then_inc(s_out_t, 1)

                over_chunks(pe, combine)

        @block.scalar
        def _(act):
            act.wait_ge(s_pool_const, POOL_CONSTANTS)
            nc.scalar.activation(act_warm[:, :], ones[:, 0:1], ACT.Gelu).then_inc(s_bias, 1)
            act.wait_ge(s_weights, 16 * WEIGHT_LOADS)
            nc.scalar.activation(gate_b2_half[:, :], gate_b2[:, :], ACT.Copy, scale=0.5).then_inc(s_bias, 1)
            act.wait_ge(s_setup_pe, 1)
            nc.scalar.activation(msg_upd[:, :], px[0:D + 1, 400:400 + D], ACT.Copy).then_inc(s_bias, 1)
            for l in range(2):
                nc.scalar.activation(mix_b_half[l][:, :], mix_b[l][:, :], ACT.Copy, scale=0.5).then_inc(s_bias, 1)
            act.wait_ge(s_bias, 5)

            def copy_transposed(c, p, semaphore):
                for k0, k1 in ((0, 4), (4, TILES_PER_CHUNK)):
                    nc.scalar.activation(h_t[p][0:D, P * k0:P * k1], pa[0:D, P * k0:P * k1], ACT.Copy).then_inc(semaphore, 1)
                for k0, k1 in ((0, 4), (4, TILES_PER_CHUNK)):
                    nc.scalar.activation(by_tile(columns(feat, c, D))[:, k0:k1, :],
                                         pa[0:D, P * k0:P * k1].rearrange("r (k p) -> r k p", p=P),
                                         ACT.Copy).then_inc(semaphore, 1)

            def evacuate(c):
                act.wait_ge(s_src_mm, c + 1)
                after(act, s_table_out, 16 * c)
                for bank, k, m in TABLE_SLOTS:
                    nc.scalar.activation(s_c[:, H2 * k:H2 * (k + m)], bank, ACT.Copy).then_inc(s_src_ev, 1)

            def source(c, p, pair):
                act.wait_ge(s_src_t, c + 1)
                after(act, s_src_mm, c - 1)
                copy_transposed(c, p, s_src_ht)
                if not is_at(c, 0):
                    evacuate(c - 1)

            act.wait_ge(s_setup, SETUP_STEPS)
            over_chunks(act, source)
            evacuate(CHUNKS - 1)

            act.wait_ge(s_ready, 1)
            rounds = load_rounds(act)

            def gelu(n, s):
                act.wait_ge(s_added, QUADS_PER_ITER * n + s + 1)
                flat = hid[s][:, :, :].rearrange("p t f -> p (t f)")
                nc.scalar.activation(flat, flat, ACT.Gelu).then_inc(s_gelu, 1)

            def tanh(n, s, free):
                act.wait_ge(s_dotted, QUADS_PER_ITER * n + s + 1)
                if free:
                    act.wait_ge(s_gated, QUADS_PER_ITER * n + s - 1)
                nc.scalar.activation(gate_t[s % 2][:, :], logit[s % 2][:, :], ACT.Tanh,
                                     bias=gate_b2_half[:, 0:1], scale=0.5).then_inc(s_tanh, 1)

            def edges(it, n, first, last):
                if first:
                    gelu(n, 0)
                    gelu(n, 1)
                    tanh(n, 0, False)
                for s in range(QUADS_PER_ITER):
                    if s + 1 < QUADS_PER_ITER:
                        tanh(n, s + 1, not (first and s == 0))
                    elif not last:
                        tanh(n + 1, 0, True)
                    if s + 2 < QUADS_PER_ITER:
                        gelu(n, s + 2)
                    elif not last:
                        gelu(n + 1, s + 2 - QUADS_PER_ITER)

            edge_pass(act, rounds, edges, lambda r: act.wait_ge(s_acc, r * GROUPS + GROUPS))

            def hidden(c):
                act.wait_ge(s_up_u, c + 1)
                after(act, s_up_mm, c)
                for i in range(2):
                    nc.scalar.activation(u_t[0:D, HALF * i:HALF * (i + 1)], pb[0:D, 512 * i:512 * i + HALF],
                                         ACT.Gelu, bias=upd_b1[:, 0:1]).then_inc(s_up_g, 1)
                nc.scalar.activation(u_t[GATE_ROW:ACC_ROWS, :], acc[GATE_ROW:ACC_ROWS, bass.ds(c * CHUNK, CHUNK)],
                                     ACT.Copy).then_inc(s_up_g, 1)

            def new_h(c, p):
                act.wait_ge(s_up_t, c + 1)
                after(act, tb[0]["mm"], c - 1)
                copy_transposed(c, p, s_up_ht)

            def update(c, p, pair):
                if not is_at(c, CHUNKS - 1):
                    hidden(c + 1)
                if not is_at(c, 0):
                    new_h(c - 1, 1 - p)

            hidden(0)
            over_chunks(act, update)
            new_h(CHUNKS - 1, (CHUNKS - 1) % 2)

            for l in range(2):
                with act.Fori(0, rounds) as r:
                    with act.Fori(0, CHUNKS) as c:
                        act.wait_ge(mx[l]["products"], r * CHUNKS + c + 1)
                        nc.scalar.activation(split(mix_c), halves(pa), ACT.Tanh, bias=mix_b_half[l][:, 0:1],
                                             scale=0.5).then_inc(mx[l]["tanh"], 1)

                if l == 0:
                    def keep(c, p, pair):
                        act.wait_ge(cb[0]["steps"], COMB_STEPS[0] * c + COMB_STEPS[0])
                        nc.scalar.activation(columns(feat, c, D), h_t[p][0:D, :], ACT.Copy).then_inc(cb[0]["kept"], 1)

                    over_chunks(act, keep)

        @block.vector
        def _(dve):
            v = nc.vector

            def layer_norm_stats(do, src, centred, squares):
                do.did(v.tensor_reduce(st[:, 0, :], tiles(src), AX.X, ALU.add))
                do.wait()
                do.did(v.tensor_scalar(st[:, 1, :], st[:, 0, :], -1.0 / D, None, ALU.mult))
                do.wait()
                do.did(v.tensor_tensor(tiles(centred), tiles(src), per_node(st[:, 1, :]), ALU.add))
                do.wait()
                do.did(v.tensor_tensor(squares, centred, centred, ALU.mult))
                do.wait()
                do.did(v.tensor_reduce(st[:, 2, :], tiles(squares), AX.X, ALU.add))
                do.wait()
                do.did(v.tensor_scalar(st[:, 3, :], st[:, 2, :], 1.0 / D, EPS, ALU.mult, ALU.add))

            do = Steps(dve, s_setup, 0)
            dve.wait_ge(s_edges, 16)
            do.did(v.tensor_copy(rel[:, :], dst_i))
            do.wait()
            by_group = rel[:, :].rearrange("p (g t) -> p g t", t=GROUP)
            do.did(v.tensor_reduce(lim[:, 0, :], by_group, AX.X, ALU.min))
            masked = dst_f
            do.did(v.scalar_tensor_tensor(out=masked, in0=rel[:, :], scalar=float(N), in1=rel[:, :],
                                          op0=ALU.is_lt, op1=ALU.mult))
            do.wait()
            do.did(v.tensor_reduce(lim[:, 1, :], masked.rearrange("p (g t) -> p g t", t=GROUP), AX.X, ALU.max))
            dve.wait_ge(s_setup_pe, 2)
            do.did(v.tensor_reduce(lim_g[:, 0, :], pa[0:GB, 0:512].rearrange("g (q p) -> g q p", p=P), AX.X, ALU.min))
            do.did(v.tensor_reduce(lim_g[:, 1, :], pb[0:GB, 0:512].rearrange("g (q p) -> g q p", p=P), AX.X, ALU.max))
            do.wait()
            do.did(v.tensor_tensor(lim_g[:, 2, :], lim_g[:, 1, :], lim_g[:, 0, :], ALU.subtract))
            do.wait()
            do.did(v.tensor_reduce(span[:, 0:1], lim_g[:, 2, :], AX.X, ALU.max))
            dve.wait_ge(s_pool_const, POOL_CONSTANTS)
            for q in range(4):
                do.did(v.tensor_scalar(diag[:, q, :], ident[0:GB, 0:GB], lim_g[:, 0, q:q + 1], None, ALU.mult))
            dve.wait_ge(s_setup_pe, 3)
            do.did(v.tensor_reduce(top[:, 0:1], sg[0][0:1, 0:GB], AX.X, ALU.max))
            do.did(v.tensor_copy(base_f[:, :], sg[1][:, 0:GROUPS]))
            do.wait()
            do.did(v.tensor_scalar(top[:, 1:2], top[:, 0:1], 0.0, None, ALU.max))
            do.did(v.tensor_copy(base_i[:, :], base_f[0:1, :]))
            do.did(v.tensor_copy(first_base[:, :], base_f[:, :]))
            do.did(v.tensor_tensor(by_group, by_group,
                                   base_f[:, :].unsqueeze(2).to_broadcast([P, GROUPS, GROUP]), ALU.subtract))
            do.wait()
            do.did(v.tensor_copy(top_i[:, 0:1], top[:, 1:2]))
            do.wait()
            do.did(v.tensor_scalar(top_i[:, 1:2], top_i[:, 0:1], WINDOW_LOG2, None, ALU.arith_shift_right))
            do.wait()
            do.did(v.tensor_scalar(rounds_i[:, :], top_i[:, 1:2], 1, None, ALU.add))
            do.did(v.tensor_copy(iota, iota_i[:, :]))
            dve.wait_ge(s_weights, 16 * WEIGHT_LOADS)
            do.wait()
            assert do.n == SETUP_STEPS
            v.tensor_copy(gate_w2_ps, gate_w2[:, :]).then_inc(s_ready, 1)

            def source(c, p, pair):
                do = Steps(dve, s_src, c * SRC_STEPS)
                h = tiles(h_c[p])
                dve.wait_ge(s_x_in[p], 16 * pair + 16)
                after(dve, s_src, c * SRC_STEPS)
                after(dve, s_h_out[p], 16 * pair)
                after(dve, s_src_t, c - 1)
                layer_norm_stats(do, x_c[p][:, :], h_c[p], t_c[:, 0:CF])
                dve.wait_ge(s_src_pow, c + 1)
                do.did(v.scalar_tensor_tensor(out=h, in0=h, scalar=0.0, in1=per_node(rstd[:, 0, :]),
                                              op0=ALU.max, op1=ALU.mult))
                assert do.n == SRC_STEPS

            over_chunks(dve, source)

            def add_window(it, n, g, rows, first, s_sum, sums, s_done):
                start = dve.value_load(base_i[0:1, bass.ds(it * GROUPS_PER_ITER + g, 1)], min_val=0, max_val=NODES)
                window = acc[0:rows, bass.ds(start, WINDOW)]
                if not first:
                    dve.wait_ge(s_done, GROUPS_PER_ITER * n + g)
                dve.wait_ge(s_sum, sums)
                v.tensor_tensor(window, window, sg[g][0:rows, 0:WINDOW], ALU.add).then_inc(s_done, 1)

            def move_windows(do):
                do.did(v.tensor_scalar(rel[:, :], rel[:, :], float(-WINDOW), None, ALU.add))
                do.did(v.tensor_scalar(base_f[:, :], base_f[:, :], float(WINDOW), float(N), ALU.add, ALU.min))
                do.wait()
                do.did(v.tensor_copy(base_i[:, :], base_f[0:1, :]))
                do.wait()

            def windows_back(s_back):
                with dve.Fori(0, rounds) as r:
                    v.tensor_scalar(rel[:, :], rel[:, :], float(WINDOW), None, ALU.add).then_inc(s_back, 1)
                    dve.wait_ge(s_back, r + 1)
                v.tensor_copy(base_f[:, :], first_base[:, :]).then_inc(s_window, 1)
                v.tensor_copy(base_i[:, :], first_base[0:1, :]).then_inc(s_window, 1)

            dve.wait_ge(s_ready, 1)
            rounds = load_rounds(dve)
            dve.wait_ge(s_acc0[0], 1)
            dve.wait_ge(s_src_ev, 4 * CHUNKS)

            def dst_quad(it, s):
                return rel[:, bass.ds(it * TILES_PER_ITER + QUAD * s, QUAD)].unsqueeze(2).to_broadcast([P, QUAD, WINDOW])

            def add(n, s):
                i = QUADS_PER_ITER * n + s
                dve.wait_ge(s_gath[s], QUAD * 16 * n + QUAD * 16)
                dve.wait_ge(s_attr_mm, i + 1)
                pair = hid[s][:, :, :].rearrange("p (b t) f -> p b (t f)", b=2)
                v.tensor_tensor(pair, attr_ps[s % 2][:, :].rearrange("p (b c) -> p b c", b=2)[:, :, 0:2 * H2], pair,
                                ALU.add).then_inc(s_added, 1)

            def dot(n, s, first):
                i = QUADS_PER_ITER * n + s
                dve.wait_ge(s_gelu, i + 1)
                if not first:
                    dve.wait_ge(s_dotted, i)
                v.tensor_tensor(prod[:, :, :], hid[s][:, :, D:H2],
                                gate_w2_ps.unsqueeze(1).to_broadcast([P, QUAD, D]), ALU.mult).then_inc(s_prod, 1)
                dve.wait_ge(s_prod, i + 1)
                v.tensor_reduce(logit[s % 2][:, :], prod[:, :, :], AX.X, ALU.add).then_inc(s_dotted, 1)

            def gate(it, n, s, free):
                i = QUADS_PER_ITER * n + s
                m = msg[s % 2]
                if free:
                    dve.wait_ge(s_seg, i - 1)
                v.tensor_tensor(hot[s % 2][:, :, :], iota.unsqueeze(1).to_broadcast([P, QUAD, WINDOW]),
                                dst_quad(it, s), ALU.is_equal)
                v.tensor_copy(m[:, :, DEG_ROW], weight[:, bass.ds(it * TILES_PER_ITER + QUAD * s, QUAD)])
                dve.wait_ge(s_tanh, i + 1)
                v.tensor_scalar(m[:, :, GATE_ROW], gate_t[s % 2][:, :], 0.5, 0.5, ALU.mult, ALU.add).then_inc(s_gcol, 1)
                dve.wait_ge(s_gcol, i + 1)
                v.tensor_tensor(m[:, :, 0:D], hid[s][:, :, 0:D],
                                m[:, :, GATE_ROW].unsqueeze(2).to_broadcast([P, QUAD, D]), ALU.mult).then_inc(s_gated, 1)

            def window_sum(it, n, g, first):
                add_window(it, n, g, ACC_ROWS, first, s_seg, QUADS_PER_ITER * n + 2 * g + 2, s_acc)

            def edges(it, n, first, last):
                if first:
                    add(n, 0)
                    add(n, 1)
                    dot(n, 0, True)
                for s in range(QUADS_PER_ITER):
                    gate(it, n, s, not (first and s < 2))
                    if s + 1 < QUADS_PER_ITER:
                        dot(n, s + 1, False)
                    elif not last:
                        dot(n + 1, 0, False)
                    if s + 2 < QUADS_PER_ITER:
                        add(n, s + 2)
                    elif not last:
                        add(n + 1, s + 2 - QUADS_PER_ITER)
                    if s == 0 and not first:
                        window_sum(it - 1, n - 1, 1, False)
                    if s == 2:
                        window_sum(it, n, 0, first)
                if last:
                    window_sum(it, n, 1, False)

            def round_end(r):
                dve.wait_ge(s_acc, r * GROUPS + GROUPS)
                move_windows(Steps(dve, s_shift, r * 3))

            edge_pass(dve, rounds, edges, round_end)
            windows_back(s_back[0])
            dve.wait_ge(s_window, 2)

            def dinv_of(c, k=0, m=TILES_PER_CHUNK):
                return dinv[:, bass.ds(c * TILES_PER_CHUNK + k, m)]

            def scale_table(c, l):
                dve.wait_ge(tb[l]["mm"], c + 1)
                after(dve, tb[l]["out"], 16 * c)
                for bank, (k, m) in zip(table_ps, NODE_SLOTS):
                    v.tensor_tensor(tiles(tab_c[:, D * k:D * (k + m)]), tiles(bank),
                                    dinv_of(c, k, m).unsqueeze(2).to_broadcast([P, m, D]),
                                    ALU.mult).then_inc(tb[l]["scaled"], 1)

            def update(c, p, pair):
                do = Steps(dve, s_up, UPD_STEPS * c)
                h, x, t = tiles(h_c[p]), tiles(x_c[p][:, :]), tiles(t_c[:, 0:CF])
                after(dve, s_up, UPD_STEPS * c)
                dve.wait_ge(s_up_in[p], 32 * pair + 32)
                dve.wait_ge(s_up_mm, c + 1)
                slots = [(tiles(bank[:, 0:(D + 1) * m], D + 1), k, k + m) for bank, (k, m) in zip(sg, NODE_SLOTS)]
                for update_and_degree, k0, k1 in slots:
                    do.did(v.tensor_tensor(h[:, k0:k1, :], update_and_degree[:, :, 0:D], h[:, k0:k1, :], ALU.add))
                for update_and_degree, k0, k1 in slots:
                    do.did(v.tensor_copy(st[:, 5, k0:k1], update_and_degree[:, :, D]))
                do.wait()
                assert do.n == UPD_READ
                layer_norm_stats(do, h_c[p], t_c[:, 0:CF], m_c[:, :])
                assert do.n == UPD_VAR1
                do.did(v.tensor_scalar(st[:, 6, :], st[:, 5, :], 0.0, None, ALU.is_gt))
                do.wait()
                do.did(v.tensor_tensor(st[:, 5, :], st[:, 5, :], st[:, 6, :], ALU.mult))
                do.did(v.tensor_scalar(st[:, 7, :], st[:, 6, :], -1.0, 1.0, ALU.mult, ALU.add))
                do.wait()
                do.did(v.tensor_tensor(st[:, 4, :], st[:, 7, :], st[:, 5, :], ALU.add))
                assert do.n == UPD_DEG
                dve.wait_ge(s_up_pow, 2 * c + 1)
                do.did(v.tensor_tensor(t, t, per_node(rstd[:, 0, :]), ALU.mult))
                do.wait()
                do.did(v.tensor_tensor(t, t, per_feature(ln_g[:, :]), ALU.mult))
                do.wait()
                do.did(v.tensor_tensor(t, t, per_feature(ln_b[:, :]), ALU.add))
                do.wait()
                do.did(v.tensor_tensor(x, x, t, ALU.add))
                do.wait()
                assert do.n == UPD_X1
                after(dve, s_up_t, c)
                layer_norm_stats(do, x_c[p][:, :], q_c, m_c[:, :])
                assert do.n == UPD_VAR2
                if not is_at(c, 0):
                    scale_table(c - 1, 0)
                dve.wait_ge(s_up_pow, 2 * c + 2)
                do.did(v.scalar_tensor_tensor(out=tiles(q_c), in0=tiles(q_c), scalar=0.0,
                                              in1=per_node(rstd[:, 0, :]), op0=ALU.max, op1=ALU.mult))
                do.did(v.tensor_tensor(dinv_of(c), rstd[:, 1, :], st[:, 6, :], ALU.mult))
                assert do.n == UPD_STEPS

            over_chunks(dve, update)
            dve.wait_ge(s_up, UPD_STEPS * CHUNKS)
            scale_table(CHUNKS - 1, 0)

            for l in range(2):
                dve.wait_ge(s_acc0[l + 1], CHUNKS)

                def conv_edges(it, n, first, last, s=cv[l]):
                    for b in range(GROUPS_PER_ITER):
                        g = GROUPS_PER_ITER * n + b
                        cols = bass.ds(it * TILES_PER_ITER + GROUP * b, GROUP)
                        if not first:
                            dve.wait_ge(s["seg"], g - 1)
                        v.tensor_tensor(conv_s[b], iota.unsqueeze(1).to_broadcast([P, GROUP, WINDOW]),
                                        rel[:, cols].unsqueeze(2).to_broadcast([P, GROUP, WINDOW]),
                                        ALU.is_equal).then_inc(s["hot"], 1)
                        dve.wait_ge(s["hot"], g + 1)
                        v.tensor_tensor(conv_s[b], conv_s[b],
                                        weight[:, cols].unsqueeze(2).to_broadcast([P, GROUP, WINDOW]),
                                        ALU.mult).then_inc(s["weighted"], 1)
                        if b == 0 and not first:
                            conv_window(it - 1, n - 1, 1, False, s)
                        if b == 1:
                            conv_window(it, n, 0, first, s)
                    if last:
                        conv_window(it, n, 1, False, s)

                def conv_window(it, n, g, first, s):
                    add_window(it, n, g, D, first, s["seg"], GROUPS_PER_ITER * n + g + 1, s["acc"])

                def conv_end(r, s=cv[l]):
                    dve.wait_ge(s["acc"], r * GROUPS + GROUPS)
                    move_windows(Steps(dve, s["shift"], r * 3))

                def mix(c, done, s=mx[l], l=l):
                    do = Steps(dve, s["steps"], done * MIX_STEPS)
                    scale, add, h = scale_c[0], add_c[0], columns(feat, c, D)
                    dve.wait_ge(s["tanh"], done + 1)
                    do.did(v.tensor_scalar(mix_c, mix_c, 0.5, 0.5, ALU.mult, ALU.add))
                    dve.wait_ge(s["dinv_in"], done * 16 + 16)
                    dve.wait_ge(s["out"], done * 32 + 32)
                    do.did(v.tensor_tensor(split(add), halves(pb), split(dinv_c), ALU.mult))
                    do.wait()
                    do.did(v.tensor_tensor(add, add, dinv_c, ALU.mult))
                    do.did(v.tensor_tensor(scale, mix_c, dinv_c, ALU.mult))
                    do.wait()
                    do.did(v.scalar_tensor_tensor(out=add, in0=add, scalar=conv_b[l][:, 0:1], in1=h,
                                                  op0=ALU.add, op1=ALU.subtract))
                    do.wait()
                    do.did(v.tensor_tensor(add, add, mix_c, ALU.mult))
                    do.wait()
                    assert do.n == MIX_STEPS
                    v.tensor_tensor(add, add, h, ALU.add).then_inc(s["done"], 1)

                edge_pass(dve, rounds, conv_edges, conv_end, mix=(None, mix, None))
                windows_back(s_back[l + 1])
                dve.wait_ge(s_window, 2 * l + 4)

                def final(c, p, pair):
                    dve.wait_ge(s_out_t, c + 1)
                    dve.wait_ge(s_x1_in[p], 16 * pair + 16)
                    after(dve, s_out, 16 * c)
                    for bank, (k, m) in zip(sg, NODE_SLOTS):
                        cols = slice(D * k, D * (k + m))
                        v.scalar_tensor_tensor(out=tab_c[:, cols], in0=bank[:, 0:D * m], scalar=0.0,
                                               in1=x_c[p][:, cols], op0=ALU.max, op1=ALU.add).then_inc(s_final, 1)

                def combine(c, p, pair, s=cb[l], l=l):
                    do = Steps(dve, s["steps"], COMB_STEPS[l] * c)
                    t, h = t_c[0:D, :], h_t[p][0:D, :]
                    after(dve, s["steps"], COMB_STEPS[l] * c)
                    dve.wait_ge(s[f"in{p}"], 32 * pair + 32)
                    do.did(v.tensor_tensor(t, columns(acc, c, D), scale_c[p], ALU.mult))
                    do.wait()
                    assert do.n == COMB_READ
                    if l == 0:
                        do.did(v.tensor_tensor(t, t, add_c[p], ALU.add))
                        do.wait()
                        after(dve, tb[1]["mm"], c - 1)
                        after(dve, s["kept"], c - 1)
                        do.did(v.tensor_scalar(h, t, 0.0, None, ALU.max))
                        if not is_at(c, 0):
                            scale_table(c - 1, 1)
                    else:
                        after(dve, s_out_t, c - 1)
                        do.did(v.tensor_tensor(h, t, add_c[p], ALU.add))
                        if not is_at(c, 0):
                            final(c - 1, 1 - p, pair - (1 - p))
                    assert do.n == COMB_STEPS[l]

                over_chunks(dve, combine)
                if l == 0:
                    scale_table(CHUNKS - 1, 1)
                else:
                    final(CHUNKS - 1, (CHUNKS - 1) % 2, (CHUNKS - 1) // 2)


def kernel(x, src, dst, edge_attr_32, edge_weight, **w):
    import numpy as np
    import concourse.bacc as bacc
    from concourse.bass_utils import run_bass_kernel_spmd

    w = {k: np.asarray(v) for k, v in w.items()}
    g, c = (lambda n: w["L0_gnn_" + n]), (lambda n: w["L1_gnn_" + n])

    def padded(a, n, fill):
        a = np.asarray(a)
        out = np.full((n,) + a.shape[1:], fill, a.dtype)
        out[:len(a)] = a
        return out

    zeros = np.zeros((1, D), np.float32)
    degree_column = np.zeros((UPD_ROWS, 1), np.float32)
    degree_column[DEG_ROW:] = 1
    row = lambda a: np.ascontiguousarray(a.reshape(1, -1))
    arrays = {
        "x": padded(x, NODES, 0).reshape(CHUNKS, P, CF),
        "src": padded(src, EDGES, 0).reshape(GROUPS, GROUP, P).transpose(0, 2, 1),
        "dst": padded(dst, EDGES, N).reshape(TILES, P).T,
        "weight": padded(edge_weight, EDGES, 0).reshape(TILES, P).T,
        "attr": padded(edge_attr_32, EDGES, 0).reshape(GROUPS, GROUP * P, ED).transpose(0, 2, 1),
        "w_src": np.concatenate([np.concatenate([g("mW1")[:D], g("gW1")[:D]], 1),
                                 np.concatenate([row(g("mb1")), row(g("gb1"))], 1)]),
        "w_attr": np.concatenate([g("mW1")[D:], g("gW1")[D:]], 1),
        "msg_w2_t": np.concatenate([g("mW2"), row(g("mb2"))]).T,
        "upd_top": g("uW1")[:D],
        "upd_bottom": g("uW1")[D:],
        "upd_b1": g("ub1").reshape(D, 1),
        "upd_w2": np.concatenate([np.concatenate([g("uW2"), zeros, zeros, row(g("ub2"))]),
                                  degree_column], 1),
        "gate_w2": row(g("gW2")),
        "gate_b2": row(g("gb2")),
        "ln_g": row(g("ln_g")),
        "ln_b": row(g("ln_b")),
    }
    for l in range(2):
        arrays[f"conv_w{l}"] = np.concatenate([c(f"W{l}"), c(f"Wr{l}")], 1)
        arrays[f"conv_b{l}"] = c(f"b{l}").reshape(D, 1)
        arrays[f"mix_b{l}"] = c(f"br{l}").reshape(D, 1)

    nc = bacc.Bacc("TRN2", target_bir_lowering=False, num_devices=1)
    in_map, io = {}, {}
    for name, a in arrays.items():
        a = np.ascontiguousarray(a)
        in_map["in_" + name] = a
        io[name] = nc.dram_tensor("in_" + name, a.shape, mybir.dt.from_np(a.dtype), kind="ExternalInput").ap()
    io["out"] = nc.dram_tensor("out_nodes", [CHUNKS, P, CF], F32, kind="ExternalOutput").ap()
    build(nc, io)
    r = run_bass_kernel_spmd(nc, [in_map], core_ids=[0])
    return r.results[0]["out_nodes"].reshape(NODES, D)[:N]
```

```python
import contextlib

import concourse.bass as bass
import concourse.mybir as mybir
from concourse.alu_op_type import AluOpType as ALU

F32 = mybir.dt.float32
I32 = mybir.dt.int32
ACT = mybir.ActivationFunctionType
AX = mybir.AxisListType

N = 12500
E = 400000
D = 96
ED = 32
P = 128
EPS = 1e-5

TILES_PER_CHUNK = 7
CHUNK = P * TILES_PER_CHUNK
CHUNKS = -(-N // CHUNK)
NODES = CHUNKS * CHUNK
CF = TILES_PER_CHUNK * D

QUAD = 4
GROUP = 8
QUADS_PER_ITER = 4
GROUPS_PER_ITER = 2
TILES_PER_ITER = QUAD * QUADS_PER_ITER
ITERS = -(-E // (P * TILES_PER_ITER))
QUADS = ITERS * QUADS_PER_ITER
GROUPS = ITERS * GROUPS_PER_ITER
TILES = ITERS * TILES_PER_ITER
EDGES = TILES * P
WINDOW = 64
WINDOW_LOG2 = 6
ACC = NODES + WINDOW
GATE_ROW = D
DEG_ROW = D + 1
ACC_ROWS = D + 2
H2 = 2 * D
GB = GROUPS // 4
WEIGHT_LOADS = 18
SETUP_STEPS = 21
POOL_CONSTANTS = 11
MIX_STEPS = 6
PAD_TILES = (EDGES - E) // P
PAD_GROUPS = -(-(EDGES - E) // (P * GROUP))
QUAD_SPARED = [min(QUAD - 1, max(0, PAD_TILES - QUAD * s)) for s in range(QUADS_PER_ITER)]
GROUP_SPARED = [min(GROUP - 1, max(0, PAD_TILES - GROUP * b)) for b in range(GROUPS_PER_ITER)]
MIX_SPAN = (ITERS - 2) // CHUNKS
MIX_AT = (0, 4, 8, MIX_SPAN)
HALF = CHUNK // 2
UPD_ROWS = D + 3


def after(engine, semaphore, value):
    if not (isinstance(value, int) and value <= 0):
        engine.wait_ge(semaphore, value)


class Steps:

    def __init__(self, engine, semaphore, base):
        self.engine, self.semaphore, self.base, self.n = engine, semaphore, base, 0

    def did(self, instruction):
        self.n += 1
        return instruction.then_inc(self.semaphore, 1)

    def wait(self):
        self.engine.wait_ge(self.semaphore, self.base + self.n)


LN_CENTRE = 3
LN_STATS = 6
FIRST_READ = 4
FIRST_STEPS = FIRST_READ + 3
SRC_COPIES = 6
DEG_STEPS = 4
SECOND_X1 = 3
SECOND_CENTRED = SECOND_X1 + LN_CENTRE
SECOND_STEPS = SECOND_CENTRED + 2
COMB_READ = 1
COMB_STEPS = [3, 2]


def build(nc, io):
    ctx = contextlib.ExitStack()
    with ctx:
        def sb(name, shape, dt=F32):
            return ctx.enter_context(nc.sbuf_tensor(name, shape, dt))

        def ps(name, columns):
            return ctx.enter_context(nc.psum_tensor(name, [P, columns], F32))

        def sem(name):
            return ctx.enter_context(nc.semaphore(name))

        def dram(name, shape):
            return nc.dram_tensor(name, shape, F32).ap()

        src_table = dram("src_table", [CHUNKS, P, TILES_PER_CHUNK * H2])
        conv_table = [dram(f"conv_table{l}", [CHUNKS, P, CF]) for l in range(2)]
        h_src = dram("h_src", [CHUNKS, P, CF])
        x1_keep = dram("x1_keep", [CHUNKS, P, CF])
        dinv_rows = dram("dinv_rows", [CHUNKS, P, TILES_PER_CHUNK])
        mix_scale = [dram(f"mix_scale{l}", [CHUNKS, D, CHUNK]) for l in range(2)]
        mix_add = [dram(f"mix_add{l}", [CHUNKS, D, CHUNK]) for l in range(2)]
        src_rows = src_table.rearrange("c p (k f) -> (c p k) f", f=H2)
        conv_rows = [t.rearrange("c p (k f) -> (c p k) f", f=D) for t in conv_table]

        acc = sb("acc", [P, ACC])
        feat = sb("feat", [P, NODES])
        rel = sb("rel", [P, TILES])
        weight = sb("weight", [P, TILES])
        base_f = sb("base_f", [P, GROUPS])
        base_i = sb("base_i", [1, GROUPS], I32)
        first_base = sb("first_base", [P, GROUPS])
        rounds_i = sb("rounds_i", [1, 1], I32)
        dinv = sb("dinv", [P, CHUNKS * TILES_PER_CHUNK])
        ident = sb("ident", [P, P])
        ones = sb("ones", [P, P])
        zero = sb("zero", [P, 1])
        centring = sb("centring", [D, D])
        w2_mean = sb("w2_mean", [UPD_ROWS, 2])
        w_src = sb("w_src", [D + 1, H2])
        w_attr = sb("w_attr", [ED, H2])
        gate_w2 = sb("gate_w2", [P, D])
        gate_b2 = sb("gate_b2", [P, 1])
        gate_b2_half = sb("gate_b2_half", [P, 1])
        msg_w2_t = sb("msg_w2_t", [D, D + 1])
        upd_top = sb("upd_top", [D, D])
        upd_bottom = sb("upd_bottom", [D, D])
        msg_upd = sb("msg_upd", [D + 1, D])
        upd_b1 = sb("upd_b1", [D, 1])
        upd_w2 = sb("upd_w2", [UPD_ROWS, D + 1])
        ln_g = sb("ln_g", [P, D])
        ln_b = sb("ln_b", [P, D])
        conv_w = [sb(f"conv_w{l}", [D, H2]) for l in range(2)]
        conv_b = [sb(f"conv_b{l}", [D, 1]) for l in range(2)]
        mix_b = [sb(f"mix_b{l}", [D, 1]) for l in range(2)]
        mix_b_half = [sb(f"mix_b_half{l}", [D, 1]) for l in range(2)]
        act_warm = sb("act_warm", [P, 1])

        x_c = [sb(f"x_c{p}", [P, CF]) for p in range(2)]
        buf_h = [sb(f"buf_h{p}", [P, CHUNK]) for p in range(2)]
        buf_b = [sb(f"buf_b{p}", [P, CHUNK]) for p in range(2)]
        t_c = sb("t_c", [P, CHUNK])
        m_c = sb("m_c", [P, CF])
        hid_all = sb("hid", [P, QUADS_PER_ITER * QUAD * H2])
        s_c = [sb("s_c0", [P, TILES_PER_CHUNK * H2])[:, :],
               hid_all[:, 0:TILES_PER_CHUNK * H2]]
        h_t = [sb(f"h_t{p}", [D + 1, CHUNK]) for p in range(2)]
        st = sb("st", [P, 12, TILES_PER_CHUNK])
        rstd = sb("rstd", [P, 3, TILES_PER_CHUNK])
        neg_half = sb("neg_half", [P, TILES_PER_CHUNK])
        h_c = [b[:, 0:CF] for b in buf_h]
        q_c = [buf_b[1][:, 0:CF], sb("buf_q", [P, CF])[:, :]]
        u_t = buf_b[0][0:UPD_ROWS, :]
        hc_c = [t_c[:, 0:CF], q_c[1]]
        centred_c = [b[:, 0:CF] for b in buf_b]
        scale_c = [b[0:D, :] for b in buf_h]
        add_c = [b[0:D, :] for b in buf_b]
        dinv_c, mix_c = scale_c[1], add_c[1]
        tab_c = s_c[0][:, 0:CF]
        src_ids = [sb(f"src_ids{b}", [P, GROUP], I32) for b in range(GROUPS_PER_ITER)]
        attr = [sb(f"attr{b}", [ED, GROUP * P]) for b in range(GROUPS_PER_ITER)]
        hid = [hid_all[:, QUAD * H2 * s:QUAD * H2 * (s + 1)].rearrange("p (t f) -> p t f", f=H2)
               for s in range(QUADS_PER_ITER)]
        prod = sb("prod", [P, QUAD, D])
        logit = [sb(f"logit{b}", [P, QUAD]) for b in range(2)]
        gate_t = [sb(f"gate_t{b}", [P, QUAD]) for b in range(2)]
        msg = [sb(f"msg{b}", [P, QUAD, ACC_ROWS]) for b in range(2)]
        hot = [sb(f"hot{b}", [P, QUAD, WINDOW]) for b in range(2)]
        hid_flat = [hid_all[:, QUAD * H2 * s:QUAD * H2 * (s + 1)] for s in range(QUADS_PER_ITER)]
        conv_g = [h.rearrange("p (t f) -> p t f", f=D) for h in hid_flat[0:2]]
        conv_s = [h[:, 0:GROUP * WINDOW].rearrange("p (t f) -> p t f", f=WINDOW) for h in hid_flat[2:4]]
        dst_f = feat[:, 0:TILES]
        dst_i = dst_f.bitcast(I32)
        lim = feat[:, TILES:TILES + 2 * GROUPS].rearrange("p (m g) -> p m g", m=2)
        iota_i = sb("iota_i", [P, WINDOW], I32)
        lim_g = sb("lim_g", [GB, 8, 4])
        diag = sb("diag", [GB, 4, GB])
        span = sb("span", [GB, 2])
        top = sb("top", [1, 2])
        top_i = sb("top_i", [1, 2], I32)

        pa = ps("pa", 1024)
        pb = ps("pb", 1024)
        sg = [ps("sg0", 512), ps("sg1", 512)]
        px = ps("px", 512)
        const = ps("const", 512)
        iota = const[:, 0:WINDOW]
        gate_w2_ps = const[:, WINDOW:WINDOW + D]
        attr_ps = [pa, pb]
        table_ps = [px[:, 0:4 * D], const[:, WINDOW + D:WINDOW + 4 * D]]

        s_weights = sem("weights_in")
        s_edges = sem("edges_in")
        s_pool_const = sem("pool_const")
        s_setup = sem("setup_steps")
        s_setup_pe = sem("setup_pe")
        s_ready = sem("setup_ready")
        s_ones = sem("u_t_ones")
        s_w2 = sem("upd_w2_centred")
        s_bias = sem("bias_ready")
        s_x_in = [sem(f"x_in{p}") for p in range(2)]
        s_src = sem("src_stats")
        s_src_h = sem("src_h")
        s_src_pow = sem("src_pow")
        s_src_t = sem("src_transposed")
        s_src_ht = sem("src_ht")
        s_src_mm = sem("src_product")
        s_src_ev = sem("src_copied")
        s_h_out = [sem(f"h_out{p}") for p in range(2)]
        s_table_out = [sem(f"table_out{p}") for p in range(2)]
        s_ids = [sem(f"ids_in{b}") for b in range(GROUPS_PER_ITER)]
        s_attr = [sem(f"attr_in{b}") for b in range(GROUPS_PER_ITER)]
        s_gath = [sem(f"gathered{s}") for s in range(QUADS_PER_ITER)]
        s_attr_mm = sem("attr_product")
        s_added = sem("added")
        s_gelu = sem("gelu_done")
        s_prod = sem("gate_products")
        s_dotted = sem("gate_logits")
        s_tanh = sem("tanh_done")
        s_gcol = sem("gate_columns")
        s_gated = sem("gated")
        s_seg = sem("segment_sums")
        s_acc = sem("accumulated")
        s_shift = sem("windows_moved")
        s_back = [sem(f"rel_back{l}") for l in range(2)]
        s_window = sem("windows_back")
        s_passed = sem("passed")
        s_round = [sem(f"round{p}_open") for p in range(3)]
        s_acc0 = [sem(f"acc_zeroed{p}") for p in range(3)]
        s_up_in = [sem(f"upd_in{p}") for p in range(2)]
        s_up_u = sem("upd_hidden")
        s_up_g = sem("upd_gelu")
        s_up_mm = sem("upd_product")
        s_first = sem("upd_first_norm")
        s_first_pow = sem("upd_first_pow")
        s_deg = sem("upd_degrees")
        s_deg_pow = sem("upd_degree_pow")
        s_dinv = sem("upd_dinv")
        s_x_b = sem("upd_x_plus_b")
        s_second = sem("upd_second_norm")
        s_second_sq = sem("upd_second_squares")
        s_second_pow = sem("upd_second_pow")
        s_up_h = sem("upd_new_h")
        s_up_t = sem("upd_transposed")
        s_up_ht = sem("upd_ht")
        s_x1_out = sem("x1_out")
        s_dinv_out = sem("dinv_out")
        tb = [{k: sem(f"table{l}_{k}") for k in ("mm", "scaled", "out")} for l in range(2)]
        cv = [{k: sem(f"conv{l}_{k}") for k in
               ("ids0", "ids1", "gath0", "gath1", "hot", "weighted", "seg", "acc", "shift")} for l in range(2)]
        mx = [{k: sem(f"mix{l}_{k}") for k in
               ("dinv_in", "gate", "own", "tanh", "steps", "done", "out")} for l in range(2)]
        cb = [{k: sem(f"comb{l}_{k}") for k in ("in0", "in1", "steps", "kept")} for l in range(2)]
        s_x1_in = [sem(f"x1_in{p}") for p in range(2)]
        s_out_t = sem("out_transposed")
        s_final = sem("out_steps")
        s_out = sem("out_stored")

        block = ctx.enter_context(nc.Block())

        def tiles(ap, f=D):
            return ap.rearrange("p (k f) -> p k f", f=f)

        def per_node(ap):
            return ap.unsqueeze(2).to_broadcast([P, TILES_PER_CHUNK, D])

        def per_feature(ap, k=TILES_PER_CHUNK):
            return ap.unsqueeze(1).to_broadcast([P, k, D])

        def chunk(t, c):
            return t[bass.ds(c, 1), :, :].rearrange("o p f -> (o p) f")

        def columns(t, c, rows):
            return t[0:rows, bass.ds(c * CHUNK, CHUNK)]

        def half_columns(t, c, i, rows):
            return t[0:rows, bass.ds(c * CHUNK + i * HALF, HALF)]

        def by_tile(ap):
            return ap.rearrange("r (p k) -> r k p", k=TILES_PER_CHUNK)

        def tile_cols(t, k, rows):
            return t[0:rows, k * P:(k + 1) * P]

        def node_cols(t, k, rows):
            return by_tile(t[0:rows, :])[:, k, :]

        def halves(ap):
            return ap[0:D, :].rearrange("r (b n) -> r b n", b=2)[:, :, 0:HALF]

        def split(ap):
            return ap.rearrange("r (b n) -> r b n", b=2)

        def table_slot(k):
            if k < 4:
                return pb[:, 512 * (k // 2) + H2 * (k % 2):512 * (k // 2) + H2 * (k % 2 + 1)]
            return sg[(k - 4) // 2][:, H2 * (k % 2):H2 * (k % 2 + 1)]

        TABLE_SLOTS = [(pb[:, 0:2 * H2], 0, 2), (pb[:, 512:512 + 2 * H2], 2, 2),
                       (sg[0][:, 0:2 * H2], 4, 2), (sg[1][:, 0:H2], 6, 1)]
        NODE_SLOTS = [(0, 4), (4, 3)]

        def node_slot(banks, k, f=D):
            return banks[k // 4][:, f * (k % 4):f * (k % 4 + 1)]

        def over_chunks(eng, body):
            for c in (0, 1):
                body(c, c, 0)
            with eng.Fori(1, CHUNKS // 2 - 1) as pair:
                c = eng.snap(pair * 2)
                body(c, 0, pair)
                body(c + 1, 1, pair)
            for c in (CHUNKS - 2, CHUNKS - 1):
                body(c, c % 2, c // 2)

        def is_at(c, *chunks):
            return isinstance(c, int) and c in chunks

        def wait_apart(eng, semaphore, value):
            eng.wait_ge(semaphore, value)
            if not isinstance(value, int):
                eng.sem_inc(s_passed, 1)

        def load_rounds(eng):
            return eng.value_load(rounds_i[0:1, 0:1], min_val=1, max_val=N // WINDOW + 1)

        def gathered(it, unit, spared):
            return it * (16 * unit) + 16 * (unit - spared)

        def gathers_back(pool, semaphores, unit, spared, s_round):
            pool.inc_swdge_sem(semaphores, [gathered(ITERS - 1, unit, less) for less in spared], mode="sub")
            pool.sem_inc(s_round, 1)

        def edge_pass(eng, rounds, iteration, round_end=None, mix=None, round_start=None):
            with eng.Fori(0, rounds) as r:
                n0 = eng.snap(r * ITERS)
                if round_start:
                    round_start(r)
                iteration(0, n0, True, False)
                if mix:
                    with eng.Fori(0, CHUNKS) as c:
                        done = eng.snap(r * CHUNKS + c)
                        i0 = eng.snap(c * MIX_SPAN + 1)
                        for i, part in enumerate(mix):
                            if part:
                                part(c, done)
                            if i + 1 < len(mix):
                                with eng.Fori(MIX_AT[i], MIX_AT[i + 1]) as j:
                                    iteration(i0 + j, n0 + i0 + j, False, False)
                with eng.Fori(CHUNKS * MIX_SPAN + 1 if mix else 1, ITERS - 1) as it:
                    iteration(it, n0 + it, False, False)
                iteration(ITERS - 1, n0 + (ITERS - 1), False, True)
                if round_end:
                    round_end(r)

        def transposes(src):
            for k in range(TILES_PER_CHUNK):
                last = nc.tensor.transpose(pa[0:D, 512 * (k // 4) + P * (k % 4):512 * (k // 4) + P * (k % 4 + 1)],
                                           src[:, k * D:(k + 1) * D], ident[:, :])
            return last

        @block.sync
        def _(sp):
            sp.dma_start(dst_i, io["dst"]).then_inc(s_edges, 16)
            for p in range(2):
                sp.dma_start(x_c[p][:, :], chunk(io["x"], p)).then_inc(s_x_in[p], 16)
            for name, t in (("w_src", w_src), ("w_attr", w_attr), ("msg_w2_t", msg_w2_t), ("upd_top", upd_top),
                            ("upd_bottom", upd_bottom), ("upd_b1", upd_b1), ("upd_w2", upd_w2),
                            ("conv_w0", conv_w[0]), ("conv_w1", conv_w[1]), ("conv_b0", conv_b[0]),
                            ("conv_b1", conv_b[1]), ("mix_b0", mix_b[0]), ("mix_b1", mix_b[1])):
                sp.dma_start(t[:, :], io[name]).then_inc(s_weights, 16)
            for name, t in (("gate_w2", gate_w2), ("gate_b2", gate_b2), ("ln_g", ln_g), ("ln_b", ln_b)):
                sp.dma_start(t[:, :], io[name].partition_broadcast(P)).then_inc(s_weights, 16)
            sp.dma_start(weight[:, :], io["weight"]).then_inc(s_weights, 16)

            def table(c, p):
                sp.wait_ge(s_src_ev, SRC_COPIES * c + SRC_COPIES)
                sp.dma_start(chunk(src_table, c), s_c[p][:, :]).then_inc(s_table_out[p], 16)
                sp.dma_start(chunk(h_src, c), hc_c[p]).then_inc(s_h_out[p], 16)

            def source(c, p, pair):
                if not is_at(c, CHUNKS - 2, CHUNKS - 1):
                    sp.wait_ge(s_src, LN_STATS * c + LN_CENTRE)
                    sp.dma_start(x_c[p][:, :], chunk(io["x"], c + 2)).then_inc(s_x_in[p], 16)
                if not is_at(c, 0, 1):
                    table(c - 2, p)

            over_chunks(sp, source)
            for c in (CHUNKS - 2, CHUNKS - 1):
                table(c, c % 2)

            def load_update(c, p):
                sp.dma_start(h_c[p], chunk(h_src, c)).then_inc(s_up_in[p], 16)
                sp.dma_start(x_c[p][:, :], chunk(io["x"], c)).then_inc(s_up_in[p], 16)

            for p in range(2):
                sp.wait_ge(s_h_out[p], 16 * (CHUNKS // 2))
            sp.wait_ge(s_src_t, CHUNKS)
            for p in range(2):
                load_update(p, p)

            sp.wait_ge(s_ready, 1)
            rounds = load_rounds(sp)

            def edges(it, n, first, last):
                for b in range(GROUPS_PER_ITER):
                    if not first:
                        for s in (2 * b, 2 * b + 1):
                            wait_apart(sp, s_gath[s], gathered(it - 1, QUAD, QUAD_SPARED[s]))
                    sp.dma_start(src_ids[b][:, :], chunk(io["src"], it * 2 + b)).then_inc(s_ids[b], 16)
                    if not first:
                        sp.wait_ge(s_attr_mm, QUADS_PER_ITER * (n - 1) + 2 * b + 2)
                    sp.dma_start(attr[b][:, :], chunk(io["attr"], it * 2 + b)).then_inc(s_attr[b], 16)

            edge_pass(sp, rounds, edges, round_start=lambda r: wait_apart(sp, s_round[0], r + 1))

            def store_table(c, l):
                sp.wait_ge(tb[l]["scaled"], 2 * c + 2)
                sp.dma_start(chunk(conv_table[l], c), tab_c).then_inc(tb[l]["out"], 16)

            def update(c, p, pair):
                sp.wait_ge(s_second, SECOND_STEPS * c + SECOND_X1)
                sp.dma_start(chunk(x1_keep, c), x_c[p][:, :]).then_inc(s_x1_out, 16)
                if not is_at(c, CHUNKS - 2, CHUNKS - 1):
                    sp.wait_ge(s_second, SECOND_STEPS * c + SECOND_CENTRED)
                    sp.wait_ge(s_x1_out, 16 * c + 16)
                    load_update(c + 2, p)
                if not is_at(c, 0):
                    store_table(c - 1, 0)

            over_chunks(sp, update)
            sp.wait_ge(s_dinv, CHUNKS)
            sp.dma_start(dinv_rows.rearrange("c p k -> p c k"),
                         dinv[:, :].rearrange("p (c k) -> p c k", k=TILES_PER_CHUNK)).then_inc(s_dinv_out, 16)
            store_table(CHUNKS - 1, 0)
            sp.wait_ge(s_x1_out, 16 * CHUNKS)

            for l in range(2):
                def conv_edges(it, n, first, last, s=cv[l]):
                    for b in range(GROUPS_PER_ITER):
                        if not first:
                            sp.wait_ge(s[f"gath{b}"], gathered(it - 1, GROUP, GROUP_SPARED[b]))
                        sp.dma_start(src_ids[b][:, :], chunk(io["src"], it * 2 + b)).then_inc(s[f"ids{b}"], 16)

                def load_dinv(c, done, s=mx[l]):
                    sp.wait_ge(s_dinv_out, 16)
                    wait_apart(sp, s["done"], done + 1)
                    row = dinv_rows[bass.ds(c, 1), :, :].rearrange("o p k -> o (p k)")
                    sp.dma_start(dinv_c, row.partition_broadcast(D)).then_inc(s["dinv_in"], 16)

                def store_mix(c, done, s=mx[l], l=l):
                    wait_apart(sp, s["done"], done + 2)
                    sp.dma_start(chunk(mix_scale[l], c), scale_c[0]).then_inc(s["out"], 16)
                    sp.dma_start(chunk(mix_add[l], c), add_c[0]).then_inc(s["out"], 16)

                def conv_end(r, l=l):
                    wait_apart(sp, mx[l]["out"], r * (32 * CHUNKS) + (32 * CHUNKS + 32))

                def load_x1(c, p):
                    sp.dma_start(x_c[p][:, :], chunk(x1_keep, c)).then_inc(s_x1_in[p], 16)

                if l == 1:
                    for p in range(2):
                        load_x1(p, p)
                sp.sem_inc(mx[l]["done"], 1)
                sp.sem_inc(mx[l]["out"], 32)
                edge_pass(sp, rounds, conv_edges, conv_end, mix=(load_dinv, None, None, store_mix),
                          round_start=lambda r, l=l: wait_apart(sp, s_round[l + 1], r + 1))

                def load_mix(c, p, s=cb[l], l=l):
                    sp.dma_start(scale_c[p], chunk(mix_scale[l], c)).then_inc(s[f"in{p}"], 16)
                    sp.dma_start(add_c[p], chunk(mix_add[l], c)).then_inc(s[f"in{p}"], 16)

                def store_out(c):
                    sp.wait_ge(s_final, 2 * c + 2)
                    sp.dma_start(chunk(io["out"], c), tab_c).then_inc(s_out, 16)

                def combine(c, p, pair, l=l):
                    sp.wait_ge(cb[l]["steps"], COMB_STEPS[l] * c + COMB_STEPS[l])
                    if not is_at(c, CHUNKS - 2, CHUNKS - 1):
                        load_mix(c + 2, p)
                    if not is_at(c, 0):
                        if l == 0:
                            store_table(c - 1, 1)
                        else:
                            store_out(c - 1)
                            if not is_at(c, CHUNKS - 1):
                                load_x1(c + 1, 1 - p)

                for p in range(2):
                    load_mix(p, p)
                over_chunks(sp, combine)
                if l == 0:
                    store_table(CHUNKS - 1, 1)
                else:
                    store_out(CHUNKS - 1)
            sp.wait_ge(s_out, 16 * CHUNKS)

        @block.gpsimd
        def _(pool):
            do = Steps(pool, s_pool_const, 0)
            for fill in (lambda: pool.memset(ident[:, :], 0.0),
                         lambda: pool.affine_select(out=ident[:, :], in_=ident[:, :], compare_op=ALU.not_equal,
                                                    fill=1.0, base=0, pattern=[[-1, P]], channel_multiplier=1),
                         lambda: pool.memset(ones[:, :], 1.0),
                         lambda: pool.iota(iota_i[:, :], pattern=[[1, WINDOW]], base=0, channel_multiplier=0),
                         lambda: pool.memset(h_t[0][D:D + 1, :], 1.0),
                         lambda: pool.memset(h_t[1][D:D + 1, :], 1.0),
                         lambda: pool.memset(hid[0][:, :, :], 0.0),
                         lambda: pool.memset(hid[1][:, :, :], 0.0),
                         lambda: pool.memset(hid[2][:, :, :], 0.0),
                         lambda: pool.memset(zero[:, :], 0.0),
                         lambda: pool.memset(neg_half[:, :], -0.5)):
                do.did(fill())
                do.wait()
            pool.memset(acc[:, :], 0.0).then_inc(s_acc0[0], 1)
            pool.wait_ge(s_acc0[0], 1)

            def inverse_root(i, out):
                return pool.tensor_tensor(rstd[:, out, :], st[:, i, :], neg_half[:, :], ALU.pow)

            def source(c, p, pair):
                pool.wait_ge(s_src, c * LN_STATS + LN_STATS)
                inverse_root(4 * p + 3, p).then_inc(s_src_pow, 1)

            over_chunks(pool, source)
            pool.wait_ge(s_src_h, CHUNKS)
            pool.memset(u_t[D:UPD_ROWS, :], 1.0).then_inc(s_ones, 1)
            pool.wait_ge(s_ones, 1)

            pool.wait_ge(s_ready, 1)
            rounds = load_rounds(pool)
            for p in range(2):
                pool.wait_ge(s_table_out[p], 16 * (CHUNKS // 2))

            def gather(it, n, first, last):
                for s in range(QUADS_PER_ITER):
                    if s % 2 == 0:
                        wait_apart(pool, s_ids[s // 2], 16 * n + 16)
                    if not first:
                        wait_apart(pool, s_gated, QUADS_PER_ITER * (n - 1) + s + 1)
                    for t in range(QUAD_SPARED[s] if first else 0, QUAD):
                        j = QUAD * (s % 2) + t
                        pool.indirect_dma_start(
                            out=hid[s][:, t, :], out_offset=None, in_=src_rows,
                            in_offset=bass.IndirectOffsetOnAxis(ap=src_ids[s // 2][:, j:j + 1], axis=0),
                        ).then_inc(s_gath[s], 16)

            def gather_end(r):
                wait_apart(pool, s_acc, r * GROUPS + GROUPS)
                gathers_back(pool, s_gath, QUAD, QUAD_SPARED, s_round[0])

            pool.sem_inc(s_round[0], 1)
            edge_pass(pool, rounds, gather, gather_end)

            def x_plus_b(c, p, pair):
                pool.wait_ge(s_up_in[p], 32 * pair + 32)
                pool.tensor_tensor(tiles(x_c[p][:, :]), tiles(x_c[p][:, :]), per_feature(ln_b[:, :]),
                                   ALU.add).then_inc(s_x_b, 1)

            def update(c, p, pair):
                pool.wait_ge(s_first, FIRST_STEPS * c + FIRST_STEPS)
                inverse_root(3, 0).then_inc(s_first_pow, 1)
                pool.wait_ge(s_deg, DEG_STEPS * c + DEG_STEPS)
                inverse_root(4, 2).then_inc(s_deg_pow, 1)
                pool.wait_ge(s_up_u, c + 1)
                pool.tensor_copy(columns(acc, c, D), zero[0:D, :].to_broadcast([D, CHUNK])).then_inc(s_acc0[1], 1)
                pool.wait_ge(s_second, SECOND_STEPS * c + SECOND_STEPS)
                inverse_root(11, 1).then_inc(s_second_pow, 1)
                if not is_at(c, CHUNKS - 1):
                    x_plus_b(c + 1, 1 - p, pair + p)

            x_plus_b(0, 0, 0)
            over_chunks(pool, update)

            for l in range(2):
                pool.wait_ge(tb[l]["out"], 16 * CHUNKS)

                def conv_gather(it, n, first, last, s=cv[l], l=l):
                    for b in range(GROUPS_PER_ITER):
                        wait_apart(pool, s[f"ids{b}"], 16 * n + 16)
                        if not first:
                            wait_apart(pool, s["seg"], GROUPS_PER_ITER * (n - 1) + b + 1)
                        for t in range(GROUP_SPARED[b] if first else 0, GROUP):
                            pool.indirect_dma_start(
                                out=conv_g[b][:, t, :], out_offset=None, in_=conv_rows[l],
                                in_offset=bass.IndirectOffsetOnAxis(ap=src_ids[b][:, t:t + 1], axis=0),
                            ).then_inc(s[f"gath{b}"], 16)

                def conv_end(r, s=cv[l], l=l):
                    wait_apart(pool, s["acc"], r * GROUPS + GROUPS)
                    gathers_back(pool, [s["gath0"], s["gath1"]], GROUP, GROUP_SPARED, s_round[l + 1])

                pool.sem_inc(s_round[l + 1], 1)
                edge_pass(pool, rounds, conv_gather, conv_end)

                if l == 0:
                    with pool.Fori(0, CHUNKS) as c:
                        pool.wait_ge(cb[0]["steps"], COMB_STEPS[0] * c + COMB_READ)
                        pool.tensor_copy(columns(acc, c, D), zero[0:D, :].to_broadcast([D, CHUNK])).then_inc(s_acc0[2], 1)

        @block.tensor
        def _(pe):
            pe.wait_ge(s_pool_const, POOL_CONSTANTS)
            pe.wait_ge(s_weights, 16 * WEIGHT_LOADS)
            nc.tensor.matmul(px[0:D + 1, 400:400 + D], msg_w2_t[:, :], upd_bottom[:, :],
                             start=True, stop=True).then_inc(s_setup_pe, 1)
            pe.wait_ge(s_setup, 5)
            for m, bank in ((0, pa), (1, pb)):
                for q in range(4):
                    last = nc.tensor.transpose(bank[0:GB, P * q:P * (q + 1)],
                                               lim[:, m, GB * q:GB * (q + 1)], ident[:, :])
            last.then_inc(s_setup_pe, 1)
            pe.wait_ge(s_setup, 13)
            nc.tensor.matmul(sg[0][0:1, 0:GB], span[:, 0:1], ident[0:GB, 0:GB], start=True, stop=True)
            for q in range(4):
                last = nc.tensor.matmul(sg[1][:, GB * q:GB * (q + 1)], ones[0:GB, :], diag[:, q, :],
                                        start=True, stop=True)
            last.then_inc(s_setup_pe, 1)

            pe.wait_ge(s_ready, 1)

            def products(c, p):
                pe.wait_ge(s_src_ht, 4 * c + 2)
                after(pe, s_src_ev, SRC_COPIES * c)
                for k in range(TILES_PER_CHUNK):
                    last = nc.tensor.matmul(table_slot(k), tile_cols(h_t[p], k, D + 1), w_src[:, :],
                                            start=True, stop=True)
                for k in range(TILES_PER_CHUNK):
                    last = nc.tensor.matmul(node_slot(table_ps, k), tile_cols(h_t[p], k, D), centring[:, :],
                                            start=True, stop=True)
                last.then_inc(s_src_mm, 1)

            def source(c, p, pair):
                pe.wait_ge(s_src_h, c + 1)
                after(pe, s_src_ht, 4 * c)
                transposes(h_c[p]).then_inc(s_src_t, 1)
                if not is_at(c, 0):
                    products(c - 1, 1 - p)

            over_chunks(pe, source)
            products(CHUNKS - 1, (CHUNKS - 1) % 2)

            rounds = load_rounds(pe)
            pe.wait_ge(s_src_ev, SRC_COPIES * CHUNKS)

            def attr_product(n, s, free):
                if s % 2 == 0:
                    pe.wait_ge(s_attr[s // 2], 16 * n + 16)
                if free:
                    pe.wait_ge(s_added, QUADS_PER_ITER * n + s - 1)
                for t in range(QUAD):
                    col = P * (QUAD * (s % 2) + t)
                    last = nc.tensor.matmul(
                        attr_ps[s % 2][:, 512 * (t // 2) + H2 * (t % 2):512 * (t // 2) + H2 * (t % 2 + 1)],
                        attr[s // 2][:, col:col + P], w_attr[:, :], start=True, stop=True)
                last.then_inc(s_attr_mm, 1)

            def edges(it, n, first, last):
                if first:
                    for s in range(3):
                        attr_product(n, s, s == 2)
                for s in range(QUADS_PER_ITER):
                    if s + 3 < QUADS_PER_ITER:
                        attr_product(n, s + 3, True)
                    elif not last:
                        attr_product(n + 1, s + 3 - QUADS_PER_ITER, True)
                    pe.wait_ge(s_gated, QUADS_PER_ITER * n + s + 1)
                    if s % 2 == 0 and not first:
                        pe.wait_ge(s_acc, GROUPS_PER_ITER * (n - 1) + s // 2 + 1)
                    for t in range(QUAD):
                        op = nc.tensor.matmul(sg[s // 2][0:ACC_ROWS, 0:WINDOW], msg[s % 2][:, t, :],
                                              hot[s % 2][:, t, :], start=(s % 2 == 0 and t == 0),
                                              stop=(s % 2 == 1 and t == QUAD - 1))
                    op.then_inc(s_seg, 1)

            edge_pass(pe, rounds, edges, lambda r: pe.wait_ge(s_acc, r * GROUPS + GROUPS))

            def hidden(c):
                for i in range(2):
                    out = pb[0:D, 512 * i:512 * i + HALF]
                    nc.tensor.matmul(out, upd_top[:, :], half_columns(feat, c, i, D), start=True, stop=False)
                    last = nc.tensor.matmul(out, msg_upd[:, :], half_columns(acc, c, i, D + 1), start=False, stop=True)
                last.then_inc(s_up_u, 1)

            def new_h(c, p):
                pe.wait_ge(s_up_h, c + 1)
                after(pe, s_up_ht, 4 * c)
                transposes(q_c[p]).then_inc(s_up_t, 1)

            def table_rows(c, p, l):
                after(pe, tb[l]["scaled"], 2 * c)
                for k in range(TILES_PER_CHUNK):
                    nodes = tile_cols(h_t[p], k, D) if l == 0 else node_cols(h_t[p], k, D)
                    last = nc.tensor.matmul(node_slot(table_ps, k), nodes, conv_w[l][:, 0:D], start=True, stop=True)
                last.then_inc(tb[l]["mm"], 1)

            def update(c, p, pair):
                pe.wait_ge(s_up_g, 3 * c + 3)
                if not is_at(c, 0):
                    pe.wait_ge(s_first, FIRST_STEPS * (c - 1) + FIRST_READ)
                for k in range(TILES_PER_CHUNK):
                    last = nc.tensor.matmul(node_slot(sg, k, D + 1), node_cols(u_t, k, UPD_ROWS), upd_w2[:, :],
                                            start=True, stop=True)
                last.then_inc(s_up_mm, 1)
                if not is_at(c, CHUNKS - 1):
                    hidden(c + 1)
                if not is_at(c, 0):
                    new_h(c - 1, 1 - p)
                    pe.wait_ge(s_up_ht, 4 * (c - 1) + 2)
                    table_rows(c - 1, 1 - p, 0)

            hidden(0)
            pe.wait_ge(s_w2, 3)
            over_chunks(pe, update)
            new_h(CHUNKS - 1, (CHUNKS - 1) % 2)
            pe.wait_ge(s_up_ht, 4 * (CHUNKS - 1) + 2)
            table_rows(CHUNKS - 1, (CHUNKS - 1) % 2, 0)

            for l in range(2):
                if l == 0:
                    pe.wait_ge(s_up_ht, 4 * CHUNKS)
                else:
                    pe.wait_ge(cb[0]["kept"], CHUNKS)

                def conv_edges(it, n, first, last, s=cv[l]):
                    for b in range(GROUPS_PER_ITER):
                        pe.wait_ge(s[f"gath{b}"], gathered(it, GROUP, GROUP_SPARED[b]))
                        pe.wait_ge(s["weighted"], GROUPS_PER_ITER * n + b + 1)
                        if not first:
                            pe.wait_ge(s["acc"], GROUPS_PER_ITER * (n - 1) + b + 1)
                        for t in range(GROUP):
                            op = nc.tensor.matmul(sg[b][0:D, 0:WINDOW], conv_g[b][:, t, :], conv_s[b][:, t, :],
                                                  start=(t == 0), stop=(t == GROUP - 1))
                        op.then_inc(s["seg"], 1)

                def mix_product(c, bank, w, signal):
                    for i in range(2):
                        last = nc.tensor.matmul(bank[0:D, 512 * i:512 * i + HALF], w, half_columns(feat, c, i, D),
                                                start=True, stop=True)
                    last.then_inc(signal, 1)

                def mix_gate(c, done, l=l):
                    wait_apart(pe, mx[l]["done"], done + 1)
                    mix_product(c, pa, conv_w[l][:, D:H2], mx[l]["gate"])

                def mix_own(c, done, l=l):
                    mix_product(c, pb, conv_w[l][:, 0:D], mx[l]["own"])

                edge_pass(pe, rounds, conv_edges, round_start=lambda r, l=l: pe.wait_ge(s_round[l + 1], r + 1),
                          mix=(mix_gate, mix_own, None, None))

                def combine(c, p, pair, l=l):
                    pe.wait_ge(cb[l]["steps"], COMB_STEPS[l] * c + COMB_STEPS[l])
                    if l == 0:
                        table_rows(c, p, 1)
                    else:
                        after(pe, s_final, 2 * c)
                        for k in range(TILES_PER_CHUNK):
                            last = nc.tensor.transpose(node_slot(sg, k), node_cols(h_t[p], k, D), ident[0:D, 0:D])
                        last.then_inc(s_out_t, 1)

                over_chunks(pe, combine)

        @block.scalar
        def _(act):
            act.wait_ge(s_pool_const, POOL_CONSTANTS)
            nc.scalar.activation(act_warm[:, :], ones[:, 0:1], ACT.Gelu).then_inc(s_bias, 1)
            act.wait_ge(s_weights, 16 * WEIGHT_LOADS)
            nc.scalar.activation(gate_b2_half[:, :], gate_b2[:, :], ACT.Copy, scale=0.5).then_inc(s_bias, 1)
            act.wait_ge(s_setup_pe, 1)
            nc.scalar.activation(msg_upd[:, :], px[0:D + 1, 400:400 + D], ACT.Copy).then_inc(s_bias, 1)
            for l in range(2):
                nc.scalar.activation(mix_b_half[l][:, :], mix_b[l][:, :], ACT.Copy, scale=0.5).then_inc(s_bias, 1)
            act.wait_ge(s_bias, 5)

            def copy_transposed(c, p, semaphore):
                for k0, k1 in ((0, 4), (4, TILES_PER_CHUNK)):
                    nc.scalar.activation(h_t[p][0:D, P * k0:P * k1], pa[0:D, P * k0:P * k1], ACT.Copy).then_inc(semaphore, 1)
                for k0, k1 in ((0, 4), (4, TILES_PER_CHUNK)):
                    nc.scalar.activation(by_tile(columns(feat, c, D))[:, k0:k1, :],
                                         pa[0:D, P * k0:P * k1].rearrange("r (k p) -> r k p", p=P),
                                         ACT.Copy).then_inc(semaphore, 1)

            def evacuate(c, p, pair):
                act.wait_ge(s_src_mm, c + 1)
                after(act, s_table_out[p], 16 * pair)
                for bank, k, m in TABLE_SLOTS:
                    nc.scalar.activation(s_c[p][:, H2 * k:H2 * (k + m)], bank, ACT.Copy).then_inc(s_src_ev, 1)
                after(act, s_h_out[p], 16 * pair)
                for bank, (k, m) in zip(table_ps, NODE_SLOTS):
                    nc.scalar.activation(hc_c[p][:, D * k:D * (k + m)], bank, ACT.Copy).then_inc(s_src_ev, 1)

            def source(c, p, pair):
                act.wait_ge(s_src_t, c + 1)
                after(act, s_src_mm, c - 1)
                copy_transposed(c, p, s_src_ht)
                if not is_at(c, 0):
                    evacuate(c - 1, 1 - p, pair - (1 - p))

            act.wait_ge(s_setup, SETUP_STEPS)
            over_chunks(act, source)
            evacuate(CHUNKS - 1, (CHUNKS - 1) % 2, CHUNKS // 2 - 1)

            act.wait_ge(s_ready, 1)
            rounds = load_rounds(act)

            def gelu(n, s):
                act.wait_ge(s_added, QUADS_PER_ITER * n + s + 1)
                flat = hid[s][:, :, :].rearrange("p t f -> p (t f)")
                nc.scalar.activation(flat, flat, ACT.Gelu).then_inc(s_gelu, 1)

            def tanh(n, s, free):
                act.wait_ge(s_dotted, QUADS_PER_ITER * n + s + 1)
                if free:
                    act.wait_ge(s_gated, QUADS_PER_ITER * n + s - 1)
                nc.scalar.activation(gate_t[s % 2][:, :], logit[s % 2][:, :], ACT.Tanh,
                                     bias=gate_b2_half[:, 0:1], scale=0.5).then_inc(s_tanh, 1)

            def edges(it, n, first, last):
                if first:
                    gelu(n, 0)
                    gelu(n, 1)
                    tanh(n, 0, False)
                for s in range(QUADS_PER_ITER):
                    if s + 1 < QUADS_PER_ITER:
                        tanh(n, s + 1, not (first and s == 0))
                    elif not last:
                        tanh(n + 1, 0, True)
                    if s + 2 < QUADS_PER_ITER:
                        gelu(n, s + 2)
                    elif not last:
                        gelu(n + 1, s + 2 - QUADS_PER_ITER)

            edge_pass(act, rounds, edges, lambda r: act.wait_ge(s_acc, r * GROUPS + GROUPS))

            def hidden(c):
                act.wait_ge(s_up_u, c + 1)
                after(act, s_up_mm, c)
                for i in range(2):
                    nc.scalar.activation(u_t[0:D, HALF * i:HALF * (i + 1)], pb[0:D, 512 * i:512 * i + HALF],
                                         ACT.Gelu, bias=upd_b1[:, 0:1]).then_inc(s_up_g, 1)
                nc.scalar.activation(u_t[GATE_ROW:ACC_ROWS, :], acc[GATE_ROW:ACC_ROWS, bass.ds(c * CHUNK, CHUNK)],
                                     ACT.Copy).then_inc(s_up_g, 1)

            def new_h(c, p):
                act.wait_ge(s_up_t, c + 1)
                after(act, tb[0]["mm"], c - 1)
                copy_transposed(c, p, s_up_ht)

            def update(c, p, pair):
                if not is_at(c, CHUNKS - 1):
                    hidden(c + 1)
                if not is_at(c, 0):
                    new_h(c - 1, 1 - p)
                act.wait_ge(s_second, SECOND_STEPS * c + SECOND_CENTRED)
                nc.scalar.activation(m_c[:, :], q_c[p], ACT.Square).then_inc(s_second_sq, 1)

            act.wait_ge(s_ones, 1)
            hidden(0)
            over_chunks(act, update)
            new_h(CHUNKS - 1, (CHUNKS - 1) % 2)

            for l in range(2):
                with act.Fori(0, rounds) as r:
                    with act.Fori(0, CHUNKS) as c:
                        act.wait_ge(mx[l]["gate"], r * CHUNKS + c + 1)
                        nc.scalar.activation(split(mix_c), halves(pa), ACT.Tanh, bias=mix_b_half[l][:, 0:1],
                                             scale=0.5).then_inc(mx[l]["tanh"], 1)

                if l == 0:
                    def keep(c, p, pair):
                        act.wait_ge(cb[0]["steps"], COMB_STEPS[0] * c + COMB_STEPS[0])
                        nc.scalar.activation(columns(feat, c, D), h_t[p][0:D, :], ACT.Copy).then_inc(cb[0]["kept"], 1)

                    over_chunks(act, keep)

        @block.vector
        def _(dve):
            v = nc.vector

            def centre(do, src, centred, i):
                do.did(v.tensor_reduce(st[:, i, :], tiles(src), AX.X, ALU.add))
                do.wait()
                do.did(v.tensor_scalar(st[:, i + 1, :], st[:, i, :], -1.0 / D, None, ALU.mult))
                do.wait()
                do.did(v.tensor_tensor(tiles(centred), tiles(src), per_node(st[:, i + 1, :]), ALU.add))

            def spread(do, squares, i):
                do.did(v.tensor_reduce(st[:, i + 2, :], tiles(squares), AX.X, ALU.add))
                do.wait()
                do.did(v.tensor_scalar(st[:, i + 3, :], st[:, i + 2, :], 1.0 / D, EPS, ALU.mult, ALU.add))

            def layer_norm_stats(do, src, centred, squares, i):
                centre(do, src, centred, i)
                do.wait()
                do.did(v.tensor_tensor(squares, centred, centred, ALU.mult))
                do.wait()
                spread(do, squares, i)

            def normed(x, inverse_root):
                return dict(in0=tiles(x), scalar=0.0, in1=per_node(inverse_root), op0=ALU.max, op1=ALU.mult)

            do = Steps(dve, s_setup, 0)
            dve.wait_ge(s_edges, 16)
            do.did(v.tensor_copy(rel[:, :], dst_i))
            do.wait()
            by_group = rel[:, :].rearrange("p (g t) -> p g t", t=GROUP)
            do.did(v.tensor_reduce(lim[:, 0, :], by_group, AX.X, ALU.min))
            do.did(v.tensor_reduce(lim[:, 1, :], by_group, AX.X, ALU.max))
            padded = rel[:, 0:PAD_GROUPS * GROUP]
            masked = dst_f[:, 0:PAD_GROUPS * GROUP]
            do.did(v.scalar_tensor_tensor(out=masked, in0=padded, scalar=float(N), in1=padded,
                                          op0=ALU.is_lt, op1=ALU.mult))
            do.wait()
            do.did(v.tensor_reduce(lim[:, 1, 0:PAD_GROUPS], masked.rearrange("p (g t) -> p g t", t=GROUP),
                                   AX.X, ALU.max))
            dve.wait_ge(s_setup_pe, 2)
            do.did(v.tensor_reduce(lim_g[:, 0, :], pa[0:GB, 0:512].rearrange("g (q p) -> g q p", p=P), AX.X, ALU.min))
            do.did(v.tensor_reduce(lim_g[:, 1, :], pb[0:GB, 0:512].rearrange("g (q p) -> g q p", p=P), AX.X, ALU.max))
            do.wait()
            do.did(v.tensor_tensor(lim_g[:, 2, :], lim_g[:, 1, :], lim_g[:, 0, :], ALU.subtract))
            do.wait()
            do.did(v.tensor_reduce(span[:, 0:1], lim_g[:, 2, :], AX.X, ALU.max))
            dve.wait_ge(s_pool_const, POOL_CONSTANTS)
            for q in range(4):
                do.did(v.tensor_scalar(diag[:, q, :], ident[0:GB, 0:GB], lim_g[:, 0, q:q + 1], None, ALU.mult))
            dve.wait_ge(s_setup_pe, 3)
            do.did(v.tensor_reduce(top[:, 0:1], sg[0][0:1, 0:GB], AX.X, ALU.max))
            do.did(v.tensor_copy(base_f[:, :], sg[1][:, 0:GROUPS]))
            do.wait()
            do.did(v.tensor_scalar(top[:, 1:2], top[:, 0:1], 0.0, None, ALU.max))
            do.wait()
            do.did(v.tensor_copy(top_i[:, 0:1], top[:, 1:2]))
            do.wait()
            do.did(v.tensor_scalar(top_i[:, 1:2], top_i[:, 0:1], WINDOW_LOG2, None, ALU.arith_shift_right))
            do.wait()
            do.did(v.tensor_scalar(rounds_i[:, :], top_i[:, 1:2], 1, None, ALU.add))
            do.did(v.tensor_copy(iota, iota_i[:, :]))
            do.did(v.tensor_scalar(centring[:, :], ident[0:D, 0:D], -1.0 / D, None, ALU.add))
            dve.wait_ge(s_weights, 16 * WEIGHT_LOADS)
            do.wait()
            assert do.n == SETUP_STEPS
            v.tensor_copy(gate_w2_ps, gate_w2[:, :]).then_inc(s_ready, 1)

            def new_source(c, p):
                dve.wait_ge(s_src_pow, c + 1)
                after(dve, s_src_t, c - 1)
                v.scalar_tensor_tensor(out=tiles(h_c[p]), **normed(centred_c[p], rstd[:, p, :])).then_inc(s_src_h, 1)

            def source(c, p, pair):
                do = Steps(dve, s_src, c * LN_STATS)
                dve.wait_ge(s_x_in[p], 16 * pair + 16)
                after(dve, s_src, c * LN_STATS)
                layer_norm_stats(do, x_c[p][:, :], centred_c[p], m_c[:, :], 4 * p)
                assert do.n == LN_STATS
                if not is_at(c, 0):
                    new_source(c - 1, 1 - p)

            over_chunks(dve, source)
            new_source(CHUNKS - 1, (CHUNKS - 1) % 2)

            def add_window(it, n, g, rows, first, s_sum, sums, s_done):
                start = dve.value_load(base_i[0:1, bass.ds(it * GROUPS_PER_ITER + g, 1)], min_val=0, max_val=NODES)
                window = acc[0:rows, bass.ds(start, WINDOW)]
                if not first:
                    dve.wait_ge(s_done, GROUPS_PER_ITER * n + g)
                dve.wait_ge(s_sum, sums)
                v.tensor_tensor(window, window, sg[g][0:rows, 0:WINDOW], ALU.add).then_inc(s_done, 1)

            def move_windows(do):
                do.did(v.tensor_scalar(rel[:, :], rel[:, :], float(-WINDOW), None, ALU.add))
                do.did(v.tensor_scalar(base_f[:, :], base_f[:, :], float(WINDOW), float(N), ALU.add, ALU.min))
                do.wait()
                do.did(v.tensor_copy(base_i[:, :], base_f[0:1, :]))
                do.wait()

            def windows_back(s_back):
                with dve.Fori(0, rounds) as r:
                    v.tensor_scalar(rel[:, :], rel[:, :], float(WINDOW), None, ALU.add).then_inc(s_back, 1)
                    dve.wait_ge(s_back, r + 1)
                v.tensor_copy(base_f[:, :], first_base[:, :]).then_inc(s_window, 1)

            dve.wait_ge(s_ready, 1)
            rounds = load_rounds(dve)
            v.tensor_scalar(first_base[:, :], base_f[:, :], float(-WINDOW), None, ALU.add).then_inc(s_window, 1)
            dve.wait_ge(s_window, 1)
            v.tensor_copy(base_f[:, :], first_base[:, :]).then_inc(s_window, 1)
            v.tensor_tensor(by_group, by_group, first_base[:, :].unsqueeze(2).to_broadcast([P, GROUPS, GROUP]),
                            ALU.subtract).then_inc(s_window, 1)
            dve.wait_ge(s_window, 3)
            v.tensor_reduce(w2_mean[:, 0:1], upd_w2[:, 0:D], AX.X, ALU.add).then_inc(s_w2, 1)
            dve.wait_ge(s_w2, 1)
            v.tensor_scalar(w2_mean[:, 1:2], w2_mean[:, 0:1], -1.0 / D, None, ALU.mult).then_inc(s_w2, 1)
            dve.wait_ge(s_w2, 2)
            v.tensor_tensor(upd_w2[:, 0:D], upd_w2[:, 0:D], w2_mean[:, 1:2].to_broadcast([UPD_ROWS, D]),
                            ALU.add).then_inc(s_w2, 1)
            dve.wait_ge(s_acc0[0], 1)
            dve.wait_ge(s_src_ev, SRC_COPIES * CHUNKS)

            def dst_quad(it, s):
                return rel[:, bass.ds(it * TILES_PER_ITER + QUAD * s, QUAD)].unsqueeze(2).to_broadcast([P, QUAD, WINDOW])

            def add(it, n, s):
                i = QUADS_PER_ITER * n + s
                dve.wait_ge(s_gath[s], gathered(it, QUAD, QUAD_SPARED[s]))
                dve.wait_ge(s_attr_mm, i + 1)
                pair = hid[s][:, :, :].rearrange("p (b t) f -> p b (t f)", b=2)
                v.tensor_tensor(pair, attr_ps[s % 2][:, :].rearrange("p (b c) -> p b c", b=2)[:, :, 0:2 * H2], pair,
                                ALU.add).then_inc(s_added, 1)

            def dot(n, s, first):
                i = QUADS_PER_ITER * n + s
                dve.wait_ge(s_gelu, i + 1)
                if not first:
                    dve.wait_ge(s_dotted, i)
                v.tensor_tensor(prod[:, :, :], hid[s][:, :, D:H2],
                                gate_w2_ps.unsqueeze(1).to_broadcast([P, QUAD, D]), ALU.mult).then_inc(s_prod, 1)
                dve.wait_ge(s_prod, i + 1)
                v.tensor_reduce(logit[s % 2][:, :], prod[:, :, :], AX.X, ALU.add).then_inc(s_dotted, 1)

            def gate(it, n, s, free):
                i = QUADS_PER_ITER * n + s
                m = msg[s % 2]
                if free:
                    dve.wait_ge(s_seg, i - 1)
                v.tensor_tensor(hot[s % 2][:, :, :], iota.unsqueeze(1).to_broadcast([P, QUAD, WINDOW]),
                                dst_quad(it, s), ALU.is_equal)
                v.tensor_copy(m[:, :, DEG_ROW], weight[:, bass.ds(it * TILES_PER_ITER + QUAD * s, QUAD)])
                dve.wait_ge(s_tanh, i + 1)
                v.tensor_scalar(m[:, :, GATE_ROW], gate_t[s % 2][:, :], 0.5, 0.5, ALU.mult, ALU.add).then_inc(s_gcol, 1)
                dve.wait_ge(s_gcol, i + 1)
                v.tensor_tensor(m[:, :, 0:D], hid[s][:, :, 0:D],
                                m[:, :, GATE_ROW].unsqueeze(2).to_broadcast([P, QUAD, D]), ALU.mult).then_inc(s_gated, 1)

            def window_sum(it, n, g, first):
                add_window(it, n, g, ACC_ROWS, first, s_seg, QUADS_PER_ITER * n + 2 * g + 2, s_acc)

            def edges(it, n, first, last):
                if first:
                    add(it, n, 0)
                    add(it, n, 1)
                    dot(n, 0, True)
                for s in range(QUADS_PER_ITER):
                    gate(it, n, s, not (first and s < 2))
                    if s + 1 < QUADS_PER_ITER:
                        dot(n, s + 1, False)
                    elif not last:
                        dot(n + 1, 0, False)
                    if s + 2 < QUADS_PER_ITER:
                        add(it, n, s + 2)
                    elif not last:
                        add(it + 1, n + 1, s + 2 - QUADS_PER_ITER)
                    if s == 0 and not first:
                        window_sum(it - 1, n - 1, 1, False)
                    if s == 2:
                        window_sum(it, n, 0, first)
                if last:
                    window_sum(it, n, 1, False)

            def edges_start(r):
                move_windows(Steps(dve, s_shift, r * 3))
                dve.wait_ge(s_round[0], r + 1)

            edge_pass(dve, rounds, edges, round_start=edges_start)

            def dinv_of(c, k=0, m=TILES_PER_CHUNK):
                return dinv[:, bass.ds(c * TILES_PER_CHUNK + k, m)]

            def scale_table(c, l):
                dve.wait_ge(tb[l]["mm"], c + 1)
                dve.wait_ge(s_dinv, c + 1)
                after(dve, tb[l]["out"], 16 * c)
                for bank, (k, m) in zip(table_ps, NODE_SLOTS):
                    v.tensor_tensor(tiles(tab_c[:, D * k:D * (k + m)]), tiles(bank),
                                    dinv_of(c, k, m).unsqueeze(2).to_broadcast([P, m, D]),
                                    ALU.mult).then_inc(tb[l]["scaled"], 1)

            def first_norm(c, p, pair):
                do = Steps(dve, s_first, FIRST_STEPS * c)
                h, t = tiles(h_c[p]), tiles(t_c[:, 0:CF])
                after(dve, s_first, FIRST_STEPS * c)
                after(dve, s_second, SECOND_STEPS * c)
                dve.wait_ge(s_up_in[p], 32 * pair + 32)
                dve.wait_ge(s_up_mm, c + 1)
                slots = [(tiles(bank[:, 0:(D + 1) * m], D + 1), k, k + m) for bank, (k, m) in zip(sg, NODE_SLOTS)]
                for update_and_degree, k0, k1 in slots:
                    do.did(v.tensor_tensor(t[:, k0:k1, :], update_and_degree[:, :, 0:D], h[:, k0:k1, :], ALU.add))
                for update_and_degree, k0, k1 in slots:
                    do.did(v.tensor_copy(st[:, 5, k0:k1], update_and_degree[:, :, D]))
                do.wait()
                assert do.n == FIRST_READ
                do.did(v.tensor_tensor(m_c[:, :], t_c[:, 0:CF], t_c[:, 0:CF], ALU.mult))
                do.wait()
                spread(do, m_c[:, :], 0)
                assert do.n == FIRST_STEPS

            def new_h(c, p):
                dve.wait_ge(s_second_pow, c + 1)
                v.scalar_tensor_tensor(out=tiles(q_c[p]), **normed(q_c[p], rstd[:, 1, :])).then_inc(s_up_h, 1)
                dve.wait_ge(s_deg_pow, c + 1)
                v.tensor_tensor(dinv_of(c), rstd[:, 2, :], st[:, 6, :], ALU.mult).then_inc(s_dinv, 1)

            def degrees(c):
                do = Steps(dve, s_deg, DEG_STEPS * c)
                after(dve, s_dinv, c)
                do.did(v.tensor_scalar(st[:, 6, :], st[:, 5, :], 0.0, None, ALU.is_gt))
                do.wait()
                do.did(v.tensor_tensor(st[:, 5, :], st[:, 5, :], st[:, 6, :], ALU.mult))
                do.did(v.tensor_scalar(st[:, 7, :], st[:, 6, :], -1.0, 1.0, ALU.mult, ALU.add))
                do.wait()
                do.did(v.tensor_tensor(st[:, 4, :], st[:, 7, :], st[:, 5, :], ALU.add))
                assert do.n == DEG_STEPS

            def second_norm(c, p):
                do = Steps(dve, s_second, SECOND_STEPS * c)
                t = tiles(t_c[:, 0:CF])
                dve.wait_ge(s_first_pow, c + 1)
                do.did(v.tensor_tensor(t, t, per_node(rstd[:, 0, :]), ALU.mult))
                do.wait()
                do.did(v.tensor_tensor(t, t, per_feature(ln_g[:, :]), ALU.mult))
                do.wait()
                dve.wait_ge(s_x_b, c + 1)
                do.did(v.tensor_tensor(x_c[p][:, :], x_c[p][:, :], t_c[:, 0:CF], ALU.add))
                do.wait()
                assert do.n == SECOND_X1
                after(dve, s_up_t, c - 1)
                centre(do, x_c[p][:, :], q_c[p], 8)
                assert do.n == SECOND_CENTRED
                if not is_at(c, 0):
                    scale_table(c - 1, 0)
                dve.wait_ge(s_second_sq, c + 1)
                spread(do, m_c[:, :], 8)
                assert do.n == SECOND_STEPS

            def update(c, p, pair):
                first_norm(c, p, pair)
                if not is_at(c, 0):
                    new_h(c - 1, 1 - p)
                degrees(c)
                second_norm(c, p)

            over_chunks(dve, update)
            new_h(CHUNKS - 1, (CHUNKS - 1) % 2)
            scale_table(CHUNKS - 1, 0)

            for l in range(2):
                dve.wait_ge(s_acc0[l + 1], CHUNKS)

                def conv_edges(it, n, first, last, s=cv[l]):
                    for b in range(GROUPS_PER_ITER):
                        g = GROUPS_PER_ITER * n + b
                        cols = bass.ds(it * TILES_PER_ITER + GROUP * b, GROUP)
                        if not first:
                            dve.wait_ge(s["seg"], g - 1)
                        v.tensor_tensor(conv_s[b], iota.unsqueeze(1).to_broadcast([P, GROUP, WINDOW]),
                                        rel[:, cols].unsqueeze(2).to_broadcast([P, GROUP, WINDOW]),
                                        ALU.is_equal).then_inc(s["hot"], 1)
                        dve.wait_ge(s["hot"], g + 1)
                        v.tensor_tensor(conv_s[b], conv_s[b],
                                        weight[:, cols].unsqueeze(2).to_broadcast([P, GROUP, WINDOW]),
                                        ALU.mult).then_inc(s["weighted"], 1)
                        if b == 0 and not first:
                            conv_window(it - 1, n - 1, 1, False, s)
                        if b == 1:
                            conv_window(it, n, 0, first, s)
                    if last:
                        conv_window(it, n, 1, False, s)

                def conv_window(it, n, g, first, s):
                    add_window(it, n, g, D, first, s["seg"], GROUPS_PER_ITER * n + g + 1, s["acc"])

                def mix(c, done, s=mx[l], l=l):
                    do = Steps(dve, s["steps"], done * MIX_STEPS)
                    scale, add, h = scale_c[0], add_c[0], columns(feat, c, D)
                    dve.wait_ge(s["tanh"], done + 1)
                    do.did(v.tensor_scalar(mix_c, mix_c, 0.5, 0.5, ALU.mult, ALU.add))
                    dve.wait_ge(s["own"], done + 1)
                    dve.wait_ge(s["dinv_in"], done * 16 + 16)
                    dve.wait_ge(s["out"], done * 32 + 32)
                    do.did(v.tensor_tensor(split(add), halves(pb), split(dinv_c), ALU.mult))
                    do.wait()
                    do.did(v.tensor_tensor(add, add, dinv_c, ALU.mult))
                    do.did(v.tensor_tensor(scale, mix_c, dinv_c, ALU.mult))
                    do.wait()
                    do.did(v.scalar_tensor_tensor(out=add, in0=add, scalar=conv_b[l][:, 0:1], in1=h,
                                                  op0=ALU.add, op1=ALU.subtract))
                    do.wait()
                    do.did(v.tensor_tensor(add, add, mix_c, ALU.mult))
                    do.wait()
                    assert do.n == MIX_STEPS
                    v.tensor_tensor(add, add, h, ALU.add).then_inc(s["done"], 1)

                windows_back(s_back[l])
                dve.wait_ge(s_window, l + 4)
                edge_pass(dve, rounds, conv_edges,
                          mix=(None, None, mix, None),
                          round_start=lambda r, s=cv[l], l=l: (
                              move_windows(Steps(dve, s["shift"], r * 3)),
                              dve.wait_ge(s_round[l + 1], r + 1)))

                def final(c, p, pair):
                    dve.wait_ge(s_out_t, c + 1)
                    dve.wait_ge(s_x1_in[p], 16 * pair + 16)
                    after(dve, s_out, 16 * c)
                    for bank, (k, m) in zip(sg, NODE_SLOTS):
                        cols = slice(D * k, D * (k + m))
                        v.scalar_tensor_tensor(out=tab_c[:, cols], in0=bank[:, 0:D * m], scalar=0.0,
                                               in1=x_c[p][:, cols], op0=ALU.max, op1=ALU.add).then_inc(s_final, 1)

                def combine(c, p, pair, s=cb[l], l=l):
                    do = Steps(dve, s["steps"], COMB_STEPS[l] * c)
                    t, h = t_c[0:D, :], h_t[p][0:D, :]
                    after(dve, s["steps"], COMB_STEPS[l] * c)
                    dve.wait_ge(s[f"in{p}"], 32 * pair + 32)
                    do.did(v.tensor_tensor(t, columns(acc, c, D), scale_c[p], ALU.mult))
                    do.wait()
                    assert do.n == COMB_READ
                    if l == 0:
                        do.did(v.tensor_tensor(t, t, add_c[p], ALU.add))
                        do.wait()
                        after(dve, tb[1]["mm"], c - 1)
                        after(dve, s["kept"], c - 1)
                        do.did(v.tensor_scalar(h, t, 0.0, None, ALU.max))
                        if not is_at(c, 0):
                            scale_table(c - 1, 1)
                    else:
                        after(dve, s_out_t, c - 1)
                        do.did(v.tensor_tensor(h, t, add_c[p], ALU.add))
                        if not is_at(c, 0):
                            final(c - 1, 1 - p, pair - (1 - p))
                    assert do.n == COMB_STEPS[l]

                over_chunks(dve, combine)
                if l == 0:
                    scale_table(CHUNKS - 1, 1)
                else:
                    final(CHUNKS - 1, (CHUNKS - 1) % 2, (CHUNKS - 1) // 2)


def kernel(x, src, dst, edge_attr_32, edge_weight, **w):
    import numpy as np
    import concourse.bacc as bacc
    from concourse.bass_utils import run_bass_kernel_spmd

    w = {k: np.asarray(v) for k, v in w.items()}
    g, c = (lambda n: w["L0_gnn_" + n]), (lambda n: w["L1_gnn_" + n])

    def padded(a, n, fill, front=False):
        a = np.asarray(a)
        out = np.full((n,) + a.shape[1:], fill, a.dtype)
        out[n - len(a) if front else 0:][:len(a)] = a
        return out

    zeros = np.zeros((1, D), np.float32)
    degree_column = np.zeros((UPD_ROWS, 1), np.float32)
    degree_column[DEG_ROW:] = 1
    row = lambda a: np.ascontiguousarray(a.reshape(1, -1))
    arrays = {
        "x": padded(x, NODES, 0).reshape(CHUNKS, P, CF),
        "src": padded(src, EDGES, 0, True).reshape(GROUPS, GROUP, P).transpose(0, 2, 1),
        "dst": padded(dst, EDGES, N, True).reshape(TILES, P).T,
        "weight": padded(edge_weight, EDGES, 0, True).reshape(TILES, P).T,
        "attr": padded(edge_attr_32, EDGES, 0, True).reshape(GROUPS, GROUP * P, ED).transpose(0, 2, 1),
        "w_src": np.concatenate([np.concatenate([g("mW1")[:D], g("gW1")[:D]], 1),
                                 np.concatenate([row(g("mb1")), row(g("gb1"))], 1)]),
        "w_attr": np.concatenate([g("mW1")[D:], g("gW1")[D:]], 1),
        "msg_w2_t": np.concatenate([g("mW2"), row(g("mb2"))]).T,
        "upd_top": g("uW1")[:D],
        "upd_bottom": g("uW1")[D:],
        "upd_b1": g("ub1").reshape(D, 1),
        "upd_w2": np.concatenate([np.concatenate([g("uW2"), zeros, zeros, row(g("ub2"))]),
                                  degree_column], 1),
        "gate_w2": row(g("gW2")),
        "gate_b2": row(g("gb2")),
        "ln_g": row(g("ln_g")),
        "ln_b": row(g("ln_b")),
    }
    for l in range(2):
        arrays[f"conv_w{l}"] = np.concatenate([c(f"W{l}"), c(f"Wr{l}")], 1)
        arrays[f"conv_b{l}"] = c(f"b{l}").reshape(D, 1)
        arrays[f"mix_b{l}"] = c(f"br{l}").reshape(D, 1)

    nc = bacc.Bacc("TRN2", target_bir_lowering=False, num_devices=1)
    in_map, io = {}, {}
    for name, a in arrays.items():
        a = np.ascontiguousarray(a)
        in_map["in_" + name] = a
        io[name] = nc.dram_tensor("in_" + name, a.shape, mybir.dt.from_np(a.dtype), kind="ExternalInput").ap()
    io["out"] = nc.dram_tensor("out_nodes", [CHUNKS, P, CF], F32, kind="ExternalOutput").ap()
    build(nc, io)
    r = run_bass_kernel_spmd(nc, [in_map], core_ids=[0])
    return r.results[0]["out_nodes"].reshape(NODES, D)[:N]
```
